# Optimizing a Trainium2 kernel written in Bass

```python
import numpy as np
import jax
import jax.numpy as jnp

def _softmax(x, axis=-1):
    return jax.nn.softmax(x, axis=axis)

def _gelu(x):
    return jax.nn.gelu(x, approximate=True)

def _silu(x):
    return jax.nn.silu(x)

def _sigmoid(x):
    return jax.nn.sigmoid(x)

def _layernorm(x, axis=-1, eps=1e-05):
    m = jnp.mean(x, axis=axis, keepdims=True)
    v = jnp.var(x, axis=axis, keepdims=True)
    return (x - m) / jnp.sqrt(v + eps)

def _scatter_add(tgt, idx, src, axis=0):
    return tgt.at[idx].add(src)

def _segment_sum(src, seg, n):
    return jax.ops.segment_sum(src, seg, n)
kernel_name = 'mk_adaln_d1_jaxref_r8_cfe1d6'

def setup_inputs(seed: int=0):
    np.random.seed(seed)
    _w = jnp.asarray

    def _L0_attn_setup():
        import jax, jax.numpy as jnp
        import numpy as np
        GROUP = 64
        MAX_REL = 32

        def _silu(x):
            return x * jax.nn.sigmoid(x)

        def _ln(x, w, b, eps=1e-05):
            m = x.mean(-1, keepdims=True)
            v = ((x - m) ** 2).mean(-1, keepdims=True)
            return (x - m) / jnp.sqrt(v + eps) * w + b

        def _rope(x):
            n, d = (x.shape[-2], x.shape[-1])
            half = d // 2
            pos = jnp.arange(n, dtype=x.dtype)
            inv_freq = 10000.0 ** (-jnp.arange(half, dtype=x.dtype) / half)
            sinusoid = pos[:, None] * inv_freq[None, :]
            sin, cos = (jnp.sin(sinusoid), jnp.cos(sinusoid))
            x1, x2 = (x[..., :half], x[..., half:])
            return jnp.concatenate([x1 * cos - x2 * sin, x2 * cos + x1 * sin], axis=-1)
        key = jax.random.key(seed)
        ks = jax.random.split(key, 8)
        B, N, D, QK, H = (4, 512, 128, 32, 256)
        s = 0.02
        return {'x': jax.random.normal(ks[0], (B, N, D), dtype=jnp.float32), 'ln1_w': jnp.ones((D,), jnp.float32), 'ln1_b': jnp.zeros((D,), jnp.float32), 'Wqk': jax.random.normal(ks[1], (QK, D), jnp.float32) * s, 'bqk': jnp.zeros((QK,), jnp.float32), 'Wv': jax.random.normal(ks[2], (H, D), jnp.float32) * s, 'bv': jnp.zeros((H,), jnp.float32), 'Wg': jax.random.normal(ks[3], (H, D), jnp.float32) * s, 'bg': jnp.zeros((H,), jnp.float32), 'Wo': jax.random.normal(ks[4], (D, H), jnp.float32) * s, 'bo': jnp.zeros((D,), jnp.float32), 'ln2_w': jnp.ones((D,), jnp.float32), 'ln2_b': jnp.zeros((D,), jnp.float32), 'gamma': jax.random.normal(ks[5], (4, QK), jnp.float32) * 0.02, 'beta': jnp.zeros((4, QK), jnp.float32), 'pos_emb': jax.random.normal(ks[6], (2 * MAX_REL + 1,), jnp.float32)}
    _L0_attn_in = _L0_attn_setup()

    def _L0_ffn_setup():
        import jax, jax.numpy as jnp
        import numpy as np
        HID, FFN, E, K = (128, 512, 8, 2)
        CAP_FACTOR = 1.25
        key = jax.random.key(seed)
        k1, k2, k3, k4 = jax.random.split(key, 4)
        B, T = (4, 256)
        x = jax.random.normal(k1, (B, T, HID), dtype=jnp.float32)
        router_w = jax.random.normal(k2, (E, HID), dtype=jnp.float32) * 0.02
        w1 = jax.random.normal(k3, (E, HID, FFN), dtype=jnp.float32) * 0.02
        w2 = jax.random.normal(k4, (E, FFN, HID), dtype=jnp.float32) * 0.02
        return {'x': x, 'router_w': router_w, 'w1': w1, 'w2': w2}
    _L0_ffn_in = _L0_ffn_setup()
    _L0_c = _w((lambda *s: np.random.randn(*s).astype(np.float32) * 0.05)(2, 128))
    _L0_wmod = _w((lambda *s: np.random.randn(*s).astype(np.float32) * 0.05)(128, 6 * 128) * 128 ** (-0.5))
    _d = {'L0_attn_x': _L0_attn_in['x'], 'L0_attn_ln1_w': _L0_attn_in['ln1_w'], 'L0_attn_ln1_b': _L0_attn_in['ln1_b'], 'L0_attn_Wqk': _L0_attn_in['Wqk'], 'L0_attn_bqk': _L0_attn_in['bqk'], 'L0_attn_Wv': _L0_attn_in['Wv'], 'L0_attn_bv': _L0_attn_in['bv'], 'L0_attn_Wg': _L0_attn_in['Wg'], 'L0_attn_bg': _L0_attn_in['bg'], 'L0_attn_Wo': _L0_attn_in['Wo'], 'L0_attn_bo': _L0_attn_in['bo'], 'L0_attn_ln2_w': _L0_attn_in['ln2_w'], 'L0_attn_ln2_b': _L0_attn_in['ln2_b'], 'L0_attn_gamma': _L0_attn_in['gamma'], 'L0_attn_beta': _L0_attn_in['beta'], 'L0_attn_pos_emb': _L0_attn_in['pos_emb'], 'L0_ffn_router_w': _L0_ffn_in['router_w'], 'L0_ffn_w1': _L0_ffn_in['w1'], 'L0_ffn_w2': _L0_ffn_in['w2'], 'L0_c': _L0_c, 'L0_wmod': _L0_wmod}
    _x0 = _d['L0_attn_x']
    _d['L0_attn_x'] = jax.random.normal(jax.random.fold_in(jax.random.key(seed), 1), (2, 2048, 128), dtype=_x0.dtype)
    del _x0
    return _d

def reference(L0_attn_x, L0_attn_ln1_w, L0_attn_ln1_b, L0_attn_Wqk, L0_attn_bqk, L0_attn_Wv, L0_attn_bv, L0_attn_Wg, L0_attn_bg, L0_attn_Wo, L0_attn_bo, L0_attn_ln2_w, L0_attn_ln2_b, L0_attn_gamma, L0_attn_beta, L0_attn_pos_emb, L0_ffn_router_w, L0_ffn_w1, L0_ffn_w2, L0_c, L0_wmod):

    def _L0_attn_ref(x, ln1_w, ln1_b, Wqk, bqk, Wv, bv, Wg, bg, Wo, bo, ln2_w, ln2_b, gamma, beta, pos_emb):
        import jax, jax.numpy as jnp
        import numpy as np
        GROUP = 64
        MAX_REL = 32

        def _silu(x):
            return x * jax.nn.sigmoid(x)

        def _ln(x, w, b, eps=1e-05):
            m = x.mean(-1, keepdims=True)
            v = ((x - m) ** 2).mean(-1, keepdims=True)
            return (x - m) / jnp.sqrt(v + eps) * w + b

        def _rope(x):
            n, d = (x.shape[-2], x.shape[-1])
            half = d // 2
            pos = jnp.arange(n, dtype=x.dtype)
            inv_freq = 10000.0 ** (-jnp.arange(half, dtype=x.dtype) / half)
            sinusoid = pos[:, None] * inv_freq[None, :]
            sin, cos = (jnp.sin(sinusoid), jnp.cos(sinusoid))
            x1, x2 = (x[..., :half], x[..., half:])
            return jnp.concatenate([x1 * cos - x2 * sin, x2 * cos + x1 * sin], axis=-1)
        b, n, d = x.shape
        G = GROUP
        x = _ln(x, ln1_w, ln1_b)
        qk = _silu(x @ Wqk.T + bqk)
        v = _silu(x @ Wv.T + bv)
        heads = qk[..., None, :] * gamma + beta
        quad_q, lin_q, quad_k, lin_k = (heads[..., i, :] for i in range(4))
        quad_q, lin_q, quad_k, lin_k = map(_rope, (quad_q, lin_q, quad_k, lin_k))
        g = n // G
        rs = lambda t: t.reshape(b, g, G, t.shape[-1])
        qq, lq, qkk, lk, vg = map(rs, (quad_q, lin_q, quad_k, lin_k, v))
        idx = jnp.arange(G)
        dist = jnp.clip(jnp.abs(idx[:, None] - idx[None, :]), 0, MAX_REL)
        bias = pos_emb[dist]
        quad_att = jnp.einsum('bgid,bgjd->bgij', qq, qkk) / G + bias
        attn = jax.nn.relu(quad_att) ** 2
        quad_out = jnp.einsum('bgij,bgje->bgie', attn, vg)
        lin_kv = jnp.einsum('bgnd,bgne->bde', lk, vg) / n
        lin_out = jnp.einsum('bgnd,bde->bgne', lq, lin_kv)
        qo = quad_out.reshape(b, n, -1)
        lo = lin_out.reshape(b, n, -1)
        gate = _silu(x @ Wg.T + bg)
        out = gate * (qo + lo)
        out = out @ Wo.T + bo
        return _ln(out, ln2_w, ln2_b)

    def _L0_ffn_ref(x, router_w, w1, w2):
        import jax, jax.numpy as jnp
        import numpy as np
        HID, FFN, E, K = (128, 512, 8, 2)
        CAP_FACTOR = 1.25
        B, T, H = x.shape
        N = B * T
        x_flat = x.reshape(N, H)
        C = max(1, int(CAP_FACTOR * N / E * K))
        logits = x_flat @ router_w.T
        probs = jax.nn.softmax(logits, axis=-1)
        top_v, top_i = jax.lax.top_k(probs, K)
        top_v = top_v / jnp.sum(top_v, axis=-1, keepdims=True)
        out = jnp.zeros_like(x_flat)
        for k in range(K):
            eid = top_i[:, k]
            gate = top_v[:, k]
            onehot = jax.nn.one_hot(eid, E, dtype=jnp.int32)
            pos = jnp.take_along_axis(jnp.cumsum(onehot, axis=0), eid[:, None], axis=1)[:, 0] - 1
            keep = pos < C
            slot = jnp.where(keep, eid * C + pos, E * C)
            buf = jnp.zeros((E * C + 1, H), dtype=x.dtype).at[slot].add(x_flat * keep[:, None].astype(x.dtype))
            expert_in = buf[:E * C].reshape(E, C, H)
            h = jax.nn.gelu(jnp.einsum('ech,ehf->ecf', expert_in, w1), approximate=False)
            y = jnp.einsum('ecf,efh->ech', h, w2)
            tok = y.reshape(E * C, H)[jnp.minimum(slot, E * C - 1)]
            out = out + tok * (gate * keep.astype(x.dtype))[:, None]
        return out.reshape(B, T, H)
    x = L0_attn_x
    mod = (_silu(L0_c) @ L0_wmod).reshape(L0_c.shape[0], 6, 1, -1)
    sa, ca, ga, sb, cb, gb = (mod[:, 0], mod[:, 1], mod[:, 2], mod[:, 3], mod[:, 4], mod[:, 5])
    ga = (2 * (ga >= 0) - 1) * jnp.maximum(jnp.abs(ga), 0.25)
    gb = (2 * (gb >= 0) - 1) * jnp.maximum(jnp.abs(gb), 0.25)
    h = _layernorm(x, axis=-1) * (1 + ca) + sa
    x = x + ga * _L0_attn_ref(h, L0_attn_ln1_w, L0_attn_ln1_b, L0_attn_Wqk, L0_attn_bqk, L0_attn_Wv, L0_attn_bv, L0_attn_Wg, L0_attn_bg, L0_attn_Wo, L0_attn_bo, L0_attn_ln2_w, L0_attn_ln2_b, L0_attn_gamma, L0_attn_beta, L0_attn_pos_emb)
    h = _layernorm(x, axis=-1) * (1 + cb) + sb
    x = x + gb * _L0_ffn_ref(h, L0_ffn_router_w, L0_ffn_w1, L0_ffn_w2)
    return x

_drawn_inputs = setup_inputs


def setup_inputs(seed=0):
    import zlib

    import numpy as np

    out = dict(_drawn_inputs(seed))
    spreads = {'L0_attn_ln1_w': (1.0, 0.2),
     'L0_attn_ln1_b': (0.0, 0.1),
     'L0_attn_bqk': (0.0, 2.0),
     'L0_attn_bv': (0.0, 0.1),
     'L0_attn_bg': (0.0, 0.1),
     'L0_attn_bo': (0.0, 0.1),
     'L0_attn_ln2_w': (1.0, 0.2),
     'L0_attn_ln2_b': (0.0, 0.294),
     'L0_attn_beta': (0.0, 2.0)}
    factors = {'L0_attn_Wqk': 39.9,
     'L0_attn_gamma': 24.457,
     'L0_ffn_router_w': 7.084,
     'L0_ffn_w1': 6.242,
     'L0_ffn_w2': 6.209}
    for name, (base, spread) in spreads.items():
        noise = np.random.default_rng([zlib.crc32(name.encode()), seed]).standard_normal(out[name].shape)
        drawn = base * np.exp(spread * noise) if base else spread * noise
        out[name] = jnp.asarray(drawn.astype(out[name].dtype))
    for name, factor in factors.items():
        out[name] = (out[name] * factor).astype(out[name].dtype)
    return out
```

```python
from contextlib import ExitStack

import concourse.bass as bass
from concourse import mybir

F32 = mybir.dt.float32
U32 = mybir.dt.uint32
ALU = mybir.AluOpType
ACT = mybir.ActivationFunctionType
AX = mybir.AxisListType

P = 128
B, N, D = 2, 2048, 128
QK, H = 32, 256
G = 64
NH = 4
E, F, K = 8, 512, 2
T = 4
UT = T * P
UB = N // UT
U = B * UB
NT = B * N // P
CAP = int(1.25 * B * N / E * K)
EB = H // P
FB = F // P
VQ = H + QK
EPS = 1e-5

C_ID, C_TRI, C_COS, C_SIN, C_EXP = 0, P, 2 * P, 2 * P + N // P * QK, 2 * P + 2 * (N // P) * QK
C_LEN = C_EXP + E
R_VQ, R_GAM, R_BET, R_BO, R_W2, R_B2 = 0, VQ, VQ + P, VQ + 2 * P, VQ + 3 * P, VQ + 4 * P
R_LEN = VQ + 5 * P


def build(nc, x, consts, rows, cols, bias, c_t, w_mod, w_vq, w_g, w_o, w_r, w_1, w_2, out):
    with ExitStack() as ctx:
        def sb(name, shape, dt=F32):
            return ctx.enter_context(nc.sbuf_tensor(name, shape, dt))

        def sem(name):
            return ctx.enter_context(nc.semaphore(name))

        X = sb("X", [P, NT, D])
        con = sb("con", [P, C_LEN])
        ident = con[:, C_ID:C_ID + P]
        tri = con[:, C_TRI:C_TRI + P]
        cos = con[:, C_COS:C_SIN].rearrange("p (t d) -> p t d", d=QK)
        sin = con[:, C_SIN:C_EXP].rearrange("p (t d) -> p t d", d=QK)
        expert_no = con[:, C_EXP:C_EXP + E]
        row = sb("row", [P, R_LEN])
        col = sb("col", [P, 4])
        bias_s = sb("bias_s", [P, G])
        cT = sb("cT", [P, B])
        wmod_s = sb("wmod_s", [P, 6 * D])
        wvq_s = sb("wvq_s", [P, VQ])
        wg_s = sb("wg_s", [P, H])
        wo_s = sb("wo_s", [P, EB, D])
        wr_s = sb("wr_s", [P, E])
        w1_s = sb("w1_s", [P, E, F])
        w2_s = sb("w2_s", [P, E, FB, D])
        ones = sb("ones", [P, P])
        half = sb("half", [P, T])
        sc = sb("sc", [P, B])
        c_rep = sb("c_rep", [P, B, P])
        mod = sb("mod", [P, B, 6, D])
        mtmp = sb("mtmp", [P, B, 2, 2, D])
        ln2w = sb("ln2w", [P, B, D])
        ln2b = sb("ln2b", [P, B, D])
        stats = sb("stats", [P, 4, 2, T, 6])
        mv = sb("mv", [P, 4, 2, T, 2])
        var = sb("var", [P, 4, 2, T])
        rstd = sb("rstd", [P, 4, 2, T])
        xn = sb("xn", [P, 2, T, D])
        z = sb("z", [P, 2, T, D])
        zT = sb("zT", [P, 2, UT])
        vq = sb("vq", [P, UB, T, VQ])
        gate = sb("gate", [P, UB, EB, UT])
        hA = sb("hA", [P, T, NH, QK])
        hB = sb("hB", [P, T, NH, QK])
        hC = sb("hC", [P, T, NH, QK])
        heads = sb("heads", [P, 2, T, NH, QK])
        qk0 = sb("qk0", [P, 2, T, P])
        headsT = sb("headsT", [P, UB, UT])
        qk0T = sb("qk0T", [P, UB, UT])
        lkv = sb("lkv", [P, B, H])
        att1 = sb("att1", [P, T, G])
        att = sb("att", [P, 2, T, P])
        go = sb("go", [P, 2, EB, UT])
        y = sb("y", [P, 2, T, D])
        yn = sb("yn", [P, 2, T, D])
        h2 = sb("h2", [P, 2, T, D])
        h2T = sb("h2T", [P, B * N])
        lts = sb("lts", [E, 2, UT])
        logits = sb("logits", [P, NT, E])
        r_max = sb("r_max", [P, NT])
        r_exp = sb("r_exp", [P, NT, E])
        r_sum = sb("r_sum", [P, NT])
        prob = sb("prob", [P, NT, E])
        top = sb("top", [P, NT, 8])
        top_i = sb("top_i", [P, NT, 8], U32)
        top_f = sb("top_f", [P, NT, K])
        g_top = sb("g_top", [P, NT, K])
        onehot = z[:, :, :, :].rearrange("p a t d -> p (a t d)")[:, 0:K * E * NT].rearrange(
            "p (k e t) -> p k e t", k=K, e=E)
        first = xn[:, :, :, :].rearrange("p a t d -> p (a t d)")[:, 0:K * E * NT]
        total = y[:, :, :, :].rearrange("p a t d -> p (a t d)")[:, 0:K * E * NT]
        run = yn[:, :, :, :].rearrange("p a t d -> p (a t d)")[:, 0:K * E * NT]
        G_te = sb("G_te", [P, E, NT])
        hid = gate[:, :, :, :].rearrange("p a b c -> p (a b c)")[:, 0:2 * FB * UT].rearrange(
            "p (s f t) -> p s f t", s=2, f=FB)
        acc = zT[:, 0, :].rearrange("p (t d) -> p t d", d=D)
        fin = zT[:, 1, :].rearrange("p (t d) -> p t d", d=D)

        bank = [ctx.enter_context(nc.psum_tensor(f"bank{i}", [P, 512], F32)) for i in range(8)]
        p_turn, p_v, p_gate, p_h, p_lkv, p_lt = bank[0], bank[1:3], bank[3], bank[4:6], bank[6], bank[7]
        p_po, p_wo, p_sc = p_h, p_gate, p_lkv

        const_in = sem("const_in"); mod_in = sem("mod_in"); proj_in = sem("proj_in"); row_in = sem("row_in")
        x_in = [sem(f"x_in{u}") for u in range(U)]
        w1_in = sem("w1_in"); w2_in = sem("w2_in")
        zeroed = sem("zeroed"); halved = sem("halved"); oned = sem("oned")
        c_silu = sem("c_silu"); c_spread = sem("c_spread"); mod_done = sem("mod_done"); mod_step = sem("mod_step")
        stat_step = sem("stat_step")
        var_ready = [sem(f"var_ready{i}") for i in range(4)]
        rstd_ready = [sem(f"rstd_ready{i}") for i in range(4)]
        xn_ready = sem("xn_ready"); u_half = sem("u_half"); u_ready = sem("u_ready"); z_ready = sem("z_ready")
        z_turned = sem("z_turned"); zt_ready = sem("zt_ready")
        vq_done = sem("vq_done"); vq_biased = sem("vq_biased"); vq_ready = sem("vq_ready")
        gate_done = sem("gate_done"); gate_ready = sem("gate_ready")
        head_step = sem("head_step"); heads_ready = sem("heads_ready"); heads_turned = sem("heads_turned")
        t1_ready = sem("t1_ready"); t2_ready = sem("t2_ready")
        lkv_done = sem("lkv_done"); lkv_ready = sem("lkv_ready")
        scores_done = sem("scores_done"); scores_biased = sem("scores_biased"); att_ready = sem("att_ready")
        po_done = sem("po_done"); go_ready = sem("go_ready"); wo_done = sem("wo_done"); y_ready = sem("y_ready")
        yn_ready = sem("yn_ready"); x2_step = sem("x2_step"); x2_ready = sem("x2_ready")
        h2n_ready = sem("h2n_ready"); h2_half = sem("h2_half"); h2_ready = sem("h2_ready")
        h2_turned = sem("h2_turned"); h2t_ready = sem("h2t_ready")
        lt_done = sem("lt_done"); lt_ready = sem("lt_ready"); logits_turned = sem("logits_turned")
        logits_ready = sem("logits_ready")
        route_step = sem("route_step"); centred = sem("centred"); exp_ready = sem("exp_ready")
        onehot_ready = sem("onehot_ready"); counted = sem("counted"); gates_ready = sem("gates_ready")
        hid_done = sem("hid_done"); hid_ready = sem("hid_ready"); y_done = sem("y_done"); y_used = sem("y_used")
        acc_step = sem("acc_step"); fin_ready = sem("fin_ready"); stored = sem("stored")

        block = ctx.enter_context(nc.Block())

        def after(eng, s, value):
            if value > 0:
                eng.wait_ge(s, value)

        @block.sync
        def _(sp):
            sp.dma_start(X[:, 0:T, :], x[0]).then_inc(x_in[0], 16)
            sp.dma_start(cT[:], c_t).then_inc(mod_in, 16)
            sp.dma_start(wmod_s[:], w_mod).then_inc(mod_in, 16)
            sp.dma_start(con[:], consts).then_inc(const_in, 16)
            sp.dma_start(row[:], rows.partition_broadcast(P)).then_inc(row_in, 16)
            sp.dma_start(col[:], cols).then_inc(proj_in, 16)
            sp.dma_start(wvq_s[:], w_vq).then_inc(proj_in, 16)
            sp.dma_start(wg_s[:], w_g).then_inc(proj_in, 16)
            for u in range(1, U):
                sp.dma_start(X[:, T * u:T * u + T, :], x[u]).then_inc(x_in[u], 16)
                if u == 1:
                    sp.dma_start(wo_s[:], w_o).then_inc(proj_in, 16)
                    sp.dma_start(wr_s[:], w_r).then_inc(proj_in, 16)
                    sp.dma_start(bias_s[:], bias).then_inc(proj_in, 16)
            sp.dma_start(w1_s[:], w_1).then_inc(w1_in, 16)
            sp.dma_start(w2_s[:], w_2).then_inc(w2_in, 16)
            with sp.Fori(0, U) as u:
                sp.wait_ge(fin_ready, u + 1)
                sp.dma_start(out[bass.ds(u, 1)].rearrange("a p t d -> (a p) t d"), fin).then_inc(stored, 16)
            sp.wait_ge(stored, 16 * U)

        @block.gpsimd
        def _(pool):
            pool.sem_inc(hid_ready, 2)
            pool.sem_inc(y_used, 2)
            pool.memset(half[:], -0.5).then_inc(halved, 1)
            pool.memset(ones[:], 1.0).then_inc(oned, 1)
            pool.memset(qk0[:], 0.0).then_inc(zeroed, 1)
            pool.memset(lkv[:], 0.0).then_inc(zeroed, 1)
            pool.memset(att[:], 0.0).then_inc(zeroed, 1)
            pool.wait_ge(halved, 1)

            def inverse_root(i, u):
                pool.wait_ge(var_ready[i], u + 1)
                pool.tensor_tensor(rstd[:, i, u % 2, :], var[:, i, u % 2, :], half[:], ALU.pow)\
                    .then_inc(rstd_ready[i], 1)

            def modulated(buf, b, scale, shift, ready, step, done, u):
                pool.wait_ge(ready, u + 1)
                if u == 0:
                    pool.wait_ge(mod_done, 1)
                pool.tensor_tensor(buf, buf, mod[:, b, scale:scale + 1, :].to_broadcast([P, T, D]), ALU.mult)\
                    .then_inc(step, 1)
                pool.wait_ge(step, u + 1)
                pool.tensor_tensor(buf, buf, mod[:, b, shift:shift + 1, :].to_broadcast([P, T, D]), ALU.add)\
                    .then_inc(done, 1)

            def residual(b, u):
                xu = X[:, T * u:T * u + T, :]
                pool.wait_ge(xn_ready, u + 1)
                pool.wait_ge(mod_done, 2)
                pool.tensor_tensor(xu, xu, ln2b[:, b:b + 1, :].to_broadcast([P, T, D]), ALU.add).then_inc(x2_step, 1)
                inverse_root(2, u)
                pool.wait_ge(yn_ready, u + 1)
                pool.tensor_tensor(yn[:, u % 2], yn[:, u % 2], ln2w[:, b:b + 1, :].to_broadcast([P, T, D]),
                                   ALU.mult).then_inc(x2_step, 1)
                pool.wait_ge(x2_step, 2 * u + 2)
                pool.tensor_tensor(xu, xu, yn[:, u % 2], ALU.add).then_inc(x2_ready, 1)

            for b in range(B):
                for g in range(UB):
                    u = UB * b + g
                    inverse_root(0, u)
                    modulated(xn[:, u % 2], b, 1, 0, xn_ready, u_half, u_ready, u)
                    inverse_root(1, u)
                for s in range(UB + 1):
                    if s < UB:
                        residual(b, UB * b + s)
                    if s >= 1:
                        u = UB * b + s - 1
                        inverse_root(3, u)
                        modulated(h2[:, u % 2], b, 4, 3, h2n_ready, h2_half, h2_ready, u)

        @block.scalar
        def _(act):
            act.wait_ge(mod_in, 32)
            act.activation(sc[:], cT[:], ACT.Silu).then_inc(c_silu, 1)
            act.wait_ge(proj_in, 48)

            def turn_z(u):
                act.wait_ge(z_turned, u + 1)
                after(act, gate_done, 2 * (u - 1))
                act.activation(zT[:, u % 2, :], p_turn[:, :], ACT.Identity, bias=col[:, 1:2], scale=col[:, 0:1])\
                    .then_inc(zt_ready, 1)

            def silu_vq(u):
                act.wait_ge(vq_biased, T * (u + 1))
                act.activation(vq[:, u % UB], vq[:, u % UB], ACT.Silu).then_inc(vq_ready, 1)

            def silu_gate(u, e):
                act.wait_ge(gate_done, EB * u + e + 1)
                after(act, go_ready, u - UB + 1)
                act.activation(gate[:, u % UB, e, :], p_gate[:, :], ACT.Silu, bias=col[:, 2 + e:3 + e])\
                    .then_inc(gate_ready, 1)

            def turn_heads(u):
                act.wait_ge(heads_turned, u + 1)
                after(act, po_done, u - UB + 1)
                act.activation(headsT[:, u % UB, :], p_h[0][:, :], ACT.Copy).then_inc(t1_ready, 1)

            def turn_h2(u):
                act.wait_ge(h2_turned, u + 1)
                act.activation(h2T[:, UT * u:UT * u + UT], p_turn[:, :], ACT.Copy).then_inc(h2t_ready, 1)

            def copy_lt(u):
                act.wait_ge(lt_done, u + 1)
                after(act, logits_turned, u - 1)
                act.activation(lts[:, u % 2, :], p_lt[0:E, :], ACT.Copy).then_inc(lt_ready, 1)

            for b in range(B):
                for s in range(UB + 1):
                    u = UB * b + s
                    if s < UB:
                        turn_z(u)
                        silu_gate(u, 0)
                        silu_gate(u, 1)
                        silu_vq(u)
                    if s >= 1:
                        turn_heads(u - 1)
                for g in range(UB):
                    u = UB * b + g
                    turn_h2(u)
                    copy_lt(u)
            act.wait_ge(centred, 1)
            act.activation(r_exp[:], r_exp[:], ACT.Exp).then_inc(exp_ready, 1)
            with act.Fori(0, U) as u:
                for e in range(E):
                    act.wait_ge(y_used, u * E + e - 1 + 2)
                    for f in range(FB):
                        act.wait_ge(hid_done, (u * E + e) * FB + f + 1)
                        act.activation(hid[:, e % 2, f, :], (p_turn, p_gate)[f % 2][:, :], ACT.Gelu)\
                            .then_inc(hid_ready, 1)

        @block.vector
        def _(dve):
            dve.wait_ge(c_silu, 1)
            dve.tensor_copy(c_rep[:], sc[:, :].unsqueeze(2).to_broadcast([P, B, P])).then_inc(c_spread, 1)
            dve.wait_ge(row_in, 16)

            def mod_vectors():
                dve.wait_ge(mod_step, 4)
                for b in range(B):
                    for j in range(2):
                        last = dve.tensor_copy(
                            mod[:, b, 3 * j:3 * j + 3, :],
                            bank[1 + 3 * b + j][:, 0:3 * D].rearrange("p (k d) -> p k d", k=3))
                last.then_inc(mod_step, 1)
                dve.wait_ge(mod_step, 5)
                dve.tensor_scalar(mtmp[:, :, :, 0, :], mod[:, :, 2::3, :], 0.0, 2.0, ALU.is_ge, ALU.mult)
                for b in range(B):
                    last = dve.scalar_tensor_tensor(out=mtmp[:, b, :, 1, :], in0=mod[:, b, 2::3, :], scalar=-1.0,
                                                    in1=mod[:, b, 2::3, :], op0=ALU.mult, op1=ALU.max)
                last.then_inc(mod_step, 1)
                dve.wait_ge(mod_step, 6)
                dve.tensor_scalar(mtmp[:, :, :, 1, :], mtmp[:, :, :, 1, :], 0.25, None, ALU.max).then_inc(mod_step, 1)
                dve.wait_ge(mod_step, 7)
                dve.tensor_scalar(mod[:, :, 1::3, :], mod[:, :, 1::3, :], 1.0, None, ALU.add).then_inc(mod_done, 1)
                dve.wait_ge(mod_done, 1)
                for b in range(B):
                    last = dve.scalar_tensor_tensor(out=mod[:, b, 2::3, :], in0=mtmp[:, b, :, 0, :], scalar=-1.0,
                                                    in1=mtmp[:, b, :, 1, :], op0=ALU.add, op1=ALU.mult)
                last.then_inc(mod_step, 1)
                dve.wait_ge(mod_step, 8)
                dve.tensor_tensor(ln2w[:], mod[:, :, 2, :], row[:, R_W2:R_W2 + D].unsqueeze(1).to_broadcast([P, B, D]), ALU.mult)
                dve.tensor_tensor(ln2b[:], mod[:, :, 2, :], row[:, R_B2:R_B2 + D].unsqueeze(1).to_broadcast([P, B, D]), ALU.mult)\
                    .then_inc(mod_done, 1)

            steps = [0]

            def stat_wait(ins):
                steps[0] += 1
                ins.then_inc(stat_step, 1)
                dve.wait_ge(stat_step, steps[0])

            def variance(i, src, u):
                after(dve, rstd_ready[i], u - 1)
                for t in range(T):
                    last = dve.bn_stats(stats[:, i, u % 2, t, :], src[:, t, :])
                stat_wait(last)
                for t in range(T):
                    last = dve.bn_aggr(mv[:, i, u % 2, t, :], stats[:, i, u % 2, t, :])
                stat_wait(last)
                dve.tensor_scalar(var[:, i, u % 2, :], mv[:, i, u % 2, :, 1], EPS, None, ALU.add)\
                    .then_inc(var_ready[i], 1)

            def normalise(i, dst, src, u, done):
                dve.wait_ge(rstd_ready[i], u + 1)
                for t in range(T):
                    last = dve.tensor_scalar(dst[:, t, :], src[:, t, :], mv[:, i, u % 2, t, 0:1],
                                             rstd[:, i, u % 2, t:t + 1], ALU.subtract, ALU.mult)
                last.then_inc(done, 1)

            def ln_x(u):
                xu = X[:, T * u:T * u + T, :]
                dve.wait_ge(x_in[u], 16)
                variance(0, xu, u)
                after(dve, z_ready, u - 1)
                normalise(0, xn[:, u % 2], xu, u, xn_ready)

            def ln_1(u):
                dve.wait_ge(u_ready, u + 1)
                variance(1, xn[:, u % 2], u)
                after(dve, z_turned, u - 1)
                normalise(1, z[:, u % 2], xn[:, u % 2], u, z_ready)

            def bias_vq(u):
                after(dve, po_done, u - UB + 1)
                for t in range(T):
                    dve.wait_ge(vq_done, T * u + t + 1)
                    dve.tensor_tensor(vq[:, u % UB, t, :], p_v[t % 2][:, 0:VQ], row[:, R_VQ:R_VQ + VQ], ALU.add)\
                        .then_inc(vq_biased, 1)

            def make_heads(u):
                g = u % UB
                n = 3 * u
                qk = vq[:, g, :, H:VQ].unsqueeze(2).to_broadcast([P, T, NH, QK])
                gam = row[:, R_GAM:R_GAM + P].rearrange("p (h d) -> p h d", h=NH).unsqueeze(1).to_broadcast([P, T, NH, QK])
                bet = row[:, R_BET:R_BET + P].rearrange("p (h d) -> p h d", h=NH).unsqueeze(1).to_broadcast([P, T, NH, QK])
                cs = cos[:, T * g:T * g + T, :].unsqueeze(2).to_broadcast([P, T, NH, QK])
                sn = sin[:, T * g:T * g + T, :].unsqueeze(2).to_broadcast([P, T, NH, QK])
                R = QK // 2
                dve.wait_ge(vq_ready, u + 1)
                dve.tensor_tensor(hA[:], qk, gam, ALU.mult).then_inc(head_step, 1)
                dve.wait_ge(head_step, n + 1)
                dve.tensor_tensor(hA[:], hA[:], bet, ALU.add).then_inc(head_step, 1)
                dve.wait_ge(head_step, n + 2)
                dve.tensor_tensor(hB[:], hA[:], cs, ALU.mult)
                dve.tensor_tensor(hC[:, :, :, 0:R], hA[:, :, :, R:QK], sn[:, :, :, 0:R], ALU.mult)
                dve.tensor_tensor(hC[:, :, :, R:QK], hA[:, :, :, 0:R], sn[:, :, :, R:QK], ALU.mult).then_inc(head_step, 1)
                dve.wait_ge(head_step, n + 3)
                after(dve, lkv_done, u - 1)
                dve.tensor_tensor(qk0[:, u % 2, :, 0:QK], hB[:, :, 2, :], hC[:, :, 2, :], ALU.add)
                dve.tensor_tensor(heads[:, u % 2], hB[:], hC[:], ALU.add).then_inc(heads_ready, 1)
                dve.wait_ge(heads_ready, u + 1)

            def turn_qk0(u):
                dve.wait_ge(heads_turned, u + 1)
                after(dve, po_done, u - UB + 1)
                dve.tensor_copy(qk0T[:, u % UB, :], p_h[1][:, :]).then_inc(t2_ready, 1)

            def scale_lkv(b):
                dve.wait_ge(lkv_done, UB * (b + 1))
                dve.tensor_scalar(lkv[QK:2 * QK, b, :], p_lkv[QK:2 * QK, 0:H], 1.0 / N, None, ALU.mult)\
                    .then_inc(lkv_ready, 1)

            def square_relu(u):
                dve.wait_ge(scores_done, u + 1)
                after(dve, att_ready, u)
                after(dve, po_done, u - 1)
                for a in range(2):
                    last = dve.scalar_tensor_tensor(
                        out=att1[G * a:G * a + G], scalar=1.0 / G,
                        in0=p_sc[G * a:G * a + G, :].rearrange("p (t i) -> p t i", t=T)[:, :, G * a:G * a + G],
                        in1=bias_s[G * a:G * a + G, :].unsqueeze(1).to_broadcast([G, T, G]),
                        op0=ALU.mult, op1=ALU.add)
                last.then_inc(scores_biased, 1)
                dve.wait_ge(scores_biased, u + 1)
                for a in range(2):
                    last = dve.scalar_tensor_tensor(
                        out=att[G * a:G * a + G, u % 2, :, G * a:G * a + G], in0=att1[G * a:G * a + G], scalar=0.0,
                        in1=att1[G * a:G * a + G], op0=ALU.max, op1=ALU.mult)
                last.then_inc(att_ready, 1)

            def gated(u):
                dve.wait_ge(po_done, u + 1)
                dve.wait_ge(gate_ready, EB * (u + 1))
                after(dve, wo_done, u - 1)
                for e in range(EB):
                    last = dve.tensor_tensor(go[:, u % 2, e, :], p_po[e][:, :], gate[:, u % UB, e, :], ALU.mult)
                last.then_inc(go_ready, 1)

            def ln_2(u):
                dve.wait_ge(wo_done, u + 1)
                after(dve, yn_ready, u - 1)
                dve.tensor_tensor(y[:, u % 2], p_wo[:, :].rearrange("p (t d) -> p t d", t=T),
                                  row[:, R_BO:R_BO + D].unsqueeze(1).to_broadcast([P, T, D]), ALU.add).then_inc(y_ready, 1)
                dve.wait_ge(y_ready, u + 1)
                variance(2, y[:, u % 2], u)
                after(dve, x2_ready, u - 1)
                normalise(2, yn[:, u % 2], y[:, u % 2], u, yn_ready)

            def ln_x2(u):
                xu = X[:, T * u:T * u + T, :]
                dve.wait_ge(x2_ready, u + 1)
                variance(3, xu, u)
                after(dve, h2_turned, u - 1)
                normalise(3, h2[:, u % 2], xu, u, h2n_ready)

            def keep_logits(u):
                dve.wait_ge(logits_turned, u + 1)
                dve.tensor_copy(logits[:, T * u:T * u + T, :],
                                p_v[0][:, 0:T * E].rearrange("p (t e) -> p t e", t=T)).then_inc(logits_ready, 1)

            mod_vectors()
            dve.wait_ge(zeroed, 3)
            for b in range(B):
                for s in range(UB + 1):
                    u = UB * b + s
                    if s < UB:
                        ln_x(u)
                        ln_1(u)
                    if s >= 1:
                        make_heads(u - 1)
                    if s < UB:
                        bias_vq(u)
                    if s >= 1:
                        turn_qk0(u - 1)
                scale_lkv(b)
                for s in range(UB + 2):
                    u = UB * b + s
                    if s < UB:
                        square_relu(u)
                    if 1 <= s <= UB:
                        gated(u - 1)
                        ln_2(u - 1)
                    if s >= 2:
                        ln_x2(u - 2)
                        keep_logits(u - 2)

            r = [0]

            def then(ins):
                r[0] += 1
                ins.then_inc(route_step, 1)
                dve.wait_ge(route_step, r[0])

            dve.wait_ge(logits_ready, U)
            then(dve.tensor_reduce(r_max[:], logits[:], AX.X, ALU.max))
            dve.tensor_tensor(r_exp[:], logits[:], r_max[:, :].unsqueeze(2).to_broadcast([P, NT, E]), ALU.subtract)\
                .then_inc(centred, 1)
            dve.wait_ge(exp_ready, 1)
            then(dve.tensor_reduce(r_sum[:], r_exp[:], AX.X, ALU.add))
            then(dve.reciprocal(r_sum[:], r_sum[:]))
            then(dve.tensor_tensor(prob[:], r_exp[:], r_sum[:, :].unsqueeze(2).to_broadcast([P, NT, E]), ALU.mult))
            for t in range(NT):
                last = dve.max(top[:, t, :], prob[:, t, :])
            then(last)
            for t in range(NT):
                last = dve.max_index(top_i[:, t, :], top[:, t, :], prob[:, t, :])
            then(last)
            dve.tensor_copy(top_f[:], top_i[:, :, 0:K])
            then(dve.tensor_reduce(r_sum[:], top[:, :, 0:K], AX.X, ALU.add))
            then(dve.reciprocal(r_sum[:], r_sum[:]))
            dve.tensor_tensor(g_top[:], top[:, :, 0:K], r_sum[:, :].unsqueeze(2).to_broadcast([P, NT, K]), ALU.mult)
            for k in range(K):
                last = dve.tensor_tensor(onehot[:, k], expert_no.unsqueeze(2).to_broadcast([P, E, NT]),
                                         top_f[:, :, k].unsqueeze(1).to_broadcast([P, E, NT]), ALU.is_equal)
            last.then_inc(onehot_ready, 1)
            dve.memset(first, 1.0).then_inc(route_step, 1)
            r[0] += 1
            dve.wait_ge(route_step, r[0])
            then(dve.memset(first.rearrange("p (j t) -> p j t", t=NT)[:, :, 0:1], 0.0))
            dve.wait_ge(counted, 1)
            then(dve.tensor_copy(total, bank[2][:, :]))
            then(dve.tensor_tensor_scan(run, first, total, 0.0, ALU.mult, ALU.add))
            then(dve.tensor_tensor(run, run, total, ALU.subtract))
            then(dve.tensor_tensor(run, run, bank[1][:, :], ALU.add))
            then(dve.scalar_tensor_tensor(out=run.rearrange("p (k e t) -> p k e t", k=K, e=E), in0=run.rearrange("p (k e t) -> p k e t", k=K, e=E),
                                          scalar=float(CAP), in1=onehot, op0=ALU.is_le, op1=ALU.mult))
            runk = run.rearrange("p (k e t) -> p k e t", k=K, e=E)
            for k in range(K):
                last = dve.tensor_tensor(onehot[:, k], runk[:, k], g_top[:, :, k].unsqueeze(1).to_broadcast([P, E, NT]), ALU.mult)
            then(last)
            dve.tensor_tensor(G_te[:], onehot[:, 0], onehot[:, 1], ALU.add).then_inc(gates_ready, 1)
            dve.wait_ge(gates_ready, 1)
            with dve.Fori(0, U) as u:
                for e in range(E):
                    dve.wait_ge(y_done, u * E + e + 1)
                    for t in range(T):
                        src = p_h[e % 2][:, P * t:P * t + P]
                        w = G_te[:, e, bass.ds(u * T + t, 1)]
                        if e == 0:
                            last = dve.tensor_scalar(acc[:, t, :], src, w, None, ALU.mult)
                        else:
                            last = dve.scalar_tensor_tensor(out=acc[:, t, :], in0=src, scalar=w, in1=acc[:, t, :],
                                                            op0=ALU.mult, op1=ALU.add)
                    last.then_inc(y_used, 1)
                    dve.wait_ge(y_used, u * E + e + 1 + 2)
                dve.wait_ge(stored, 16 * u)
                dve.tensor_tensor(acc, acc, mod[:, bass.ds(u // UB, 1), 5, :].to_broadcast([P, T, D]), ALU.mult).then_inc(acc_step, 1)
                dve.wait_ge(acc_step, u + 1)
                dve.tensor_tensor(fin, acc, X[:, bass.ds(u * T, T), :], ALU.add).then_inc(fin_ready, 1)
                dve.wait_ge(fin_ready, u + 1)

        @block.tensor
        def _(pe):
            pe.wait_ge(c_spread, 1)
            pe.wait_ge(mod_in, 32)
            for b in range(B):
                for j in range(2):
                    pe.matmul(bank[1 + 3 * b + j][:, 0:3 * D], c_rep[:, b, :], wmod_s[:, 3 * D * j:3 * D * (j + 1)],
                              start=True, stop=True).then_inc(mod_step, 1)
            pe.wait_ge(const_in, 16)
            pe.wait_ge(proj_in, 96)
            pe.wait_ge(mod_step, 5)

            def turn_z(u):
                pe.wait_ge(z_ready, u + 1)
                after(pe, zt_ready, u)
                after(pe, h2t_ready, u // UB * UB)
                for t in range(T):
                    last = pe.transpose(p_turn[:, P * t:P * t + P], z[:, u % 2, t, :], ident)
                last.then_inc(z_turned, 1)

            def project(u):
                pe.wait_ge(zt_ready, u + 1)
                after(pe, logits_ready, u // UB * UB)
                after(pe, y_ready, u // UB * UB)
                for e in range(EB):
                    after(pe, gate_ready, EB * u + e)
                    pe.matmul(p_gate[:, :], wg_s[:, P * e:P * e + P], zT[:, u % 2, :], start=True, stop=True)\
                        .then_inc(gate_done, 1)
                    for t in range(2 * e, 2 * e + 2):
                        after(pe, vq_biased, T * u + t - 1)
                        pe.matmul(p_v[t % 2][:, 0:VQ], zT[:, u % 2, P * t:P * t + P], wvq_s[:], start=True, stop=True)\
                            .then_inc(vq_done, 1)

            def turn_heads(u):
                pe.wait_ge(heads_ready, u + 1)
                after(pe, t1_ready, u)
                after(pe, t2_ready, u)
                after(pe, go_ready, u // UB * UB)
                after(pe, scores_biased, u // UB * UB)
                for t in range(T):
                    pe.transpose(p_h[0][:, P * t:P * t + P], heads[:, u % 2, t].rearrange("p h d -> p (h d)"), ident)
                    last = pe.transpose(p_h[1][:, P * t:P * t + P], qk0[:, u % 2, t, :], ident)
                last.then_inc(heads_turned, 1)
                for t in range(T):
                    last = pe.matmul(p_lkv[QK:2 * QK, 0:H], heads[:, u % 2, t, 3, :], vq[:, u % UB, t, 0:H],
                                     start=(u % UB == 0 and t == 0), stop=(u % UB == UB - 1 and t == T - 1))
                last.then_inc(lkv_done, 1)

            def scores(u):
                pe.wait_ge(t1_ready, u + 1)
                pe.wait_ge(t2_ready, u + 1)
                pe.wait_ge(lkv_ready, u // UB + 1)
                after(pe, scores_biased, u)
                for t in range(T):
                    last = pe.matmul(p_sc[:, P * t:P * t + P], qk0T[:, u % UB, P * t:P * t + P],
                                     headsT[:, u % UB, P * t:P * t + P], start=True, stop=True)
                last.then_inc(scores_done, 1)

            def attend(u):
                b = u // UB
                pe.wait_ge(t1_ready, (b + 1) * UB)
                pe.wait_ge(t2_ready, (b + 1) * UB)
                after(pe, go_ready, u)
                pe.wait_ge(att_ready, u + 1)
                for e in range(EB):
                    for t in range(T):
                        tile = p_po[e][:, P * t:P * t + P]
                        pe.matmul(tile, lkv[:, b, P * e:P * e + P], headsT[:, u % UB, P * t:P * t + P],
                                  start=True, stop=False)
                        last = pe.matmul(tile, vq[:, u % UB, t, P * e:P * e + P], att[:, u % 2, t, :],
                                         start=False, stop=True)
                last.then_inc(po_done, 1)

            def project_out(u):
                pe.wait_ge(go_ready, u + 1)
                after(pe, gate_ready, EB * (u // UB + 1) * UB)
                after(pe, y_ready, u)
                for t in range(T):
                    for e in range(EB):
                        last = pe.matmul(p_wo[:, P * t:P * t + P], go[:, u % 2, e, P * t:P * t + P], wo_s[:, e, :],
                                         start=(e == 0), stop=(e == EB - 1))
                last.then_inc(wo_done, 1)

            def turn_h2(u):
                pe.wait_ge(h2_ready, u + 1)
                after(pe, zt_ready, (u // UB + 1) * UB)
                after(pe, h2t_ready, u)
                for t in range(T):
                    last = pe.transpose(p_turn[:, P * t:P * t + P], h2[:, u % 2, t, :], ident)
                last.then_inc(h2_turned, 1)

            def route(u):
                pe.wait_ge(h2t_ready, u + 1)
                after(pe, lt_ready, u)
                pe.matmul(p_lt[0:E, :], wr_s[:], h2T[:, UT * u:UT * u + UT], start=True, stop=True).then_inc(lt_done, 1)
                pe.wait_ge(lt_ready, u + 1)
                after(pe, logits_ready, u)
                after(pe, vq_biased, T * UB * (u // UB + 1))
                for t in range(T):
                    last = pe.transpose(p_v[0][:, E * t:E * t + E], lts[:, u % 2, P * t:P * t + P], ident[0:E, 0:E])
                last.then_inc(logits_turned, 1)

            for b in range(B):
                for s in range(UB + 1):
                    u = UB * b + s
                    if s < UB:
                        turn_z(u)
                        project(u)
                    if s >= 1:
                        turn_heads(u - 1)
                for s in range(UB + 2):
                    u = UB * b + s
                    if s < UB:
                        scores(u)
                    if 1 <= s <= UB:
                        attend(u - 1)
                        project_out(u - 1)
                    if s >= 2:
                        turn_h2(u - 2)
                        route(u - 2)

            pe.wait_ge(onehot_ready, 1)
            pe.wait_ge(oned, 1)
            flat = onehot.rearrange("p k e t -> p (k e t)")
            pe.matmul(bank[1][:, :], tri, flat, start=True, stop=True)
            pe.matmul(bank[2][:, :], ones[:], flat, start=True, stop=True).then_inc(counted, 1)

            pe.wait_ge(w1_in, 16)
            pe.wait_ge(w2_in, 16)
            with pe.Fori(0, U) as u:
                for e in range(E):
                    for f in range(FB):
                        pe.wait_ge(hid_ready, (u * E + e) * FB + f - 1 + 2)
                        pe.matmul((p_turn, p_gate)[f % 2][:, :], w1_s[:, e, P * f:P * f + P], h2T[:, bass.ds(u * UT, UT)],
                                  start=True, stop=True).then_inc(hid_done, 1)
                    pe.wait_ge(hid_ready, (u * E + e + 1) * FB + 2)
                    pe.wait_ge(y_used, u * E + e - 1 + 2)
                    for t in range(T):
                        for f in range(FB):
                            last = pe.matmul(p_h[e % 2][:, P * t:P * t + P], hid[:, e % 2, f, P * t:P * t + P], w2_s[:, e, f, :],
                                             start=(f == 0), stop=(f == FB - 1))
                    last.then_inc(y_done, 1)


def kernel(**inputs):
    import numpy as np
    import concourse.bacc as bacc
    from concourse import mybir as mb
    from concourse.bass_utils import run_bass_kernel_spmd

    a = {k: np.asarray(v) for k, v in inputs.items()}
    at = lambda n: a["L0_attn_" + n]
    half = QK // 2
    freq = (np.float32(10000.0) ** (-np.arange(half, dtype=np.float32) / np.float32(half))).astype(np.float32)
    ang = np.arange(N, dtype=np.float32)[:, None] * freq[None, :]
    cos = np.concatenate([np.cos(ang), np.cos(ang)], 1).reshape(N // P, P, QK).transpose(1, 0, 2).reshape(P, -1)
    sin = np.concatenate([-np.sin(ang), np.sin(ang)], 1).reshape(N // P, P, QK).transpose(1, 0, 2).reshape(P, -1)
    consts = np.concatenate([np.eye(P), np.triu(np.ones((P, P))), cos, sin,
                             np.tile(np.arange(E), (P, 1))], 1).astype(np.float32)
    rows = np.concatenate([at("bv"), at("bqk"), at("gamma").ravel(), at("beta").ravel(), at("bo"),
                           at("ln2_w"), at("ln2_b")])
    cols = np.stack([at("ln1_w"), at("ln1_b"), at("bg")[:P], at("bg")[P:]], 1)
    i = np.arange(G)
    bias = at("pos_emb")[np.minimum(np.abs(i[:, None] - i[None, :]), at("pos_emb").shape[0] // 2)]
    arrays = {
        "x": at("x").reshape(U, T, P, D).transpose(0, 2, 1, 3),
        "consts": consts,
        "rows": rows,
        "cols": cols,
        "bias": np.concatenate([bias, bias], 0),
        "c_t": a["L0_c"].T,
        "w_mod": a["L0_wmod"],
        "w_vq": np.concatenate([at("Wv").T, at("Wqk").T], 1),
        "w_g": at("Wg").T,
        "w_o": at("Wo").T.reshape(EB, P, D).transpose(1, 0, 2),
        "w_r": a["L0_ffn_router_w"].T,
        "w_1": a["L0_ffn_w1"].transpose(1, 0, 2),
        "w_2": a["L0_ffn_w2"].reshape(E, FB, P, D).transpose(2, 0, 1, 3),
    }
    arrays = {k: np.ascontiguousarray(v) for k, v in arrays.items()}
    nc = bacc.Bacc("TRN2", target_bir_lowering=False, num_devices=1)
    args = [nc.dram_tensor(k, v.shape, mb.dt.from_np(v.dtype), kind="ExternalInput").ap() for k, v in arrays.items()]
    out = nc.dram_tensor("out", (U, P, T, D), mb.dt.float32, kind="ExternalOutput").ap()
    build(nc, *args, out)
    r = run_bass_kernel_spmd(nc, [arrays], core_ids=[0])
    return r.results[0]["out"].reshape(U, P, T, D).transpose(0, 2, 1, 3).reshape(B, N, D)
```

```python
from contextlib import ExitStack

import concourse.bass as bass
from concourse import mybir

F32 = mybir.dt.float32
BF16 = mybir.dt.bfloat16
I32 = mybir.dt.int32
U32 = mybir.dt.uint32
ALU = mybir.AluOpType
ACT = mybir.ActivationFunctionType
AX = mybir.AxisListType

P = 128
B, N, D = 2, 2048, 128
QK, H = 32, 256
G = 64
NH = 4
E, F, K = 8, 512, 2
T = 4
UT = T * P
UB = N // UT
U = B * UB
NT = B * N // P
CAP = int(1.25 * B * N / E * K)
EB = H // P
FB = F // P
VQ = H + QK
EPS = 1e-5

PITCH = 2 * CAP + P
SPARE = E * PITCH
SLOTS = 4
NB = -(-(K * B * N // P + E) // SLOTS) * SLOTS
ROW = D + 4
NOWHERE = 1 << 20

C_ID, C_TRI, C_COS = 0, P, 2 * P
C_SIN = C_COS + N // P * QK
C_EXP = C_SIN + N // P * QK
C_TOK = C_EXP + E
C_BLK = C_TOK + NT
C_BASE = C_BLK + NB
C_LEN = C_BASE + E
R_VQ, R_GAM, R_BET, R_BO, R_W2, R_B2 = 0, VQ, VQ + P, VQ + 2 * P, VQ + 3 * P, VQ + 4 * P
R_LEN = VQ + 5 * P


def order():
    def project_slot(b, s):
        u = UB * b + s
        own = b == 0
        if own and s + 1 < UB:
            yield "stats_x", u + 1
        if s < UB:
            if own:
                yield "norm_u", u
            yield "project", u
        if 1 <= s <= UB:
            yield "heads", u - 1
        if own and s + 1 < UB:
            yield "norm_x", u + 1
        if s < UB:
            yield "values", u
        if 1 <= s <= UB:
            yield "turn_heads", u - 1
        if own and s + 1 < UB:
            yield "stats_u", u + 1

    def attend_slot(b, s):
        u = UB * b + s
        front = u + UB if b == 0 and s < UB else None
        if s < UB:
            yield "scores", u
        if 1 <= s <= UB:
            yield "attend", u - 1
        if 3 <= s <= UB + 2:
            yield "norm_x2", u - 3
        if front is not None:
            yield "stats_x", front
        if 2 <= s <= UB + 1:
            yield "project_out", u - 2
        if front is not None:
            yield "norm_x", front
        if 3 <= s <= UB + 2:
            yield "logits", u - 3
        if 2 <= s <= UB + 1:
            yield "norm_y", u - 2
        if front is not None:
            yield "stats_u", front
        if 3 <= s <= UB + 2:
            yield "places", u - 3
        if 2 <= s <= UB + 1:
            yield "stats_x2", u - 2
        if front is not None:
            yield "norm_u", front

    yield "stats_x", 0
    yield "norm_x", 0
    yield "stats_u", 0
    for s in range(UB + 1):
        yield from project_slot(0, s)
    yield "linear", 0
    for s in range(UB):
        yield from attend_slot(0, s)
    for s in range(UB + 1):
        if s < 3:
            yield from attend_slot(0, UB + s)
        yield from project_slot(1, s)
    yield "linear", 1
    for s in range(UB + 3):
        yield from attend_slot(1, s)


def build(nc, x, consts, rows, cols, bias, c_t, w_mod, w_vq, w_g, w_o, w_r, w_1, w_2, out):
    with ExitStack() as ctx:
        def sb(name, shape, dt=F32):
            return ctx.enter_context(nc.sbuf_tensor(name, shape, dt))

        def sem(name):
            return ctx.enter_context(nc.semaphore(name))

        to_experts = nc.dram_tensor("to_experts", (SPARE + P, ROW), F32, kind="Internal").ap()
        from_experts = nc.dram_tensor("from_experts", (K * B * N, D), F32, kind="Internal").ap()

        X = sb("X", [P, NT, D])
        con = sb("con", [P, C_LEN])
        ident = con[:, C_ID:C_ID + P]
        cos = con[:, C_COS:C_SIN].rearrange("p (t d) -> p t d", d=QK)
        sin = con[:, C_SIN:C_EXP].rearrange("p (t d) -> p t d", d=QK)
        expert_no = con[:, C_EXP:C_TOK]
        token_mark = con[:, C_TOK:C_BLK]
        block_row = con[:, C_BLK:C_BASE]
        expert_row = con[:, C_BASE:C_LEN]
        row = sb("row", [P, R_LEN])
        col = sb("col", [P, 4])
        bias_s = sb("bias_s", [P, G])
        cT = sb("cT", [P, B])
        wmod_s = sb("wmod_s", [P, 6 * D])
        wvq_s = sb("wvq_s", [P, VQ])
        wg_s = sb("wg_s", [P, H])
        wo_s = sb("wo_s", [P, EB, D])
        wr_s = sb("wr_s", [P, E])
        w1_s = sb("w1_s", [P, E, F])
        w2_s = sb("w2_s", [P, E, FB, D])
        tri16 = sb("tri16", [P, P], BF16)
        ones16 = sb("ones16", [P, P], BF16)
        half = sb("half", [P, T])
        pad = sb("pad", [P, ROW])
        sc = sb("sc", [P, B])
        c_rep = sb("c_rep", [P, B, P])
        mod = sb("mod", [P, B, 6, D])
        mtmp = sb("mtmp", [P, B, 2, 2, D])
        ln2w = sb("ln2w", [P, B, D])
        ln2b = sb("ln2b", [P, B, D])
        stats = sb("stats", [P, 4, 2, T, 6])
        mv = sb("mv", [P, 4, 2, T, 2])
        var = sb("var", [P, 4, 2, T])
        rstd = sb("rstd", [P, 4, 2, T])
        minus = sb("minus", [P, 2, 2, T])
        nmr = sb("nmr", [P, 2, 2, T])
        xn = sb("xn", [P, 2, T, D])
        z = sb("z", [P, UB, T, D])
        zT = sb("zT", [P, 2, UT])
        vq = sb("vq", [P, UB, T, VQ])
        gate = sb("gate", [P, UB, EB, UT])
        hA = sb("hA", [P, T, NH, QK])
        hB = sb("hB", [P, T, NH, QK])
        hC = sb("hC", [P, T, NH, QK])
        heads = sb("heads", [P, 2, T, NH, QK])
        qk0 = sb("qk0", [P, 2, T, P])
        headsT = sb("headsT", [P, UB, UT])
        qk0T = sb("qk0T", [P, UB, UT])
        lkv = sb("lkv", [P, B, H])
        att1 = sb("att1", [P, T, G])
        att = sb("att", [P, 2, T, P])
        go = sb("go", [P, 2, EB, UT])
        y = sb("y", [P, 2, T, D])
        yn = sb("yn", [P, 2, T, D])
        hx = sb("hx", [P, NT, ROW])
        h2T = sb("h2T", [P, UT])
        top = sb("top", [P, 2, T, 8])
        top_i = sb("top_i", [P, 2, T, 8], U32)
        first_e = sb("first_e", [P, 2, T, K])
        oh = sb("oh", [P, 2, T, K, E], BF16)
        before = sb("before", [P, NT + 1, K, E], BF16)
        gap = sb("gap", [P, 2, T])
        lean = sb("lean", [P, 2, T])
        picked = sb("picked", [P, T, K, E])
        place = sb("place", [P, T, K])
        far = sb("far", [P, T, K])
        side = sb("side", [P, T, K])
        base = sb("base", [P, T, K])
        target = sb("target", [P, U, T, K], U32)
        cnt = sb("cnt", [P, K, E])
        cnt_all = sb("cnt_all", [P, E])
        cnt_i = sb("cnt_i", [P, E], I32)
        ends = sb("ends", [P, E])
        one_e = sb("one_e", [P, E])
        start_row = sb("start_row", [P, E])
        pad_row = sb("pad_row", [P, E], I32)
        blk_e = sb("blk_e", [P, NB])
        blk_ei = sb("blk_ei", [P, NB], I32)
        blk_r = sb("blk_r", [P, NB])
        blk_ri = sb("blk_ri", [P, NB], I32)
        own_e = sb("own_e", [P, SLOTS])
        is_first = sb("is_first", [P, SLOTS])
        weight = sb("weight", [P, SLOTS])
        dest = sb("dest", [P, SLOTS], U32)
        w1_b = heads[:].rearrange("p a t h d -> p a (t h d)")
        hid = qk0[:].rearrange("p a t d -> p a (t d)")
        xb = xn[:].rearrange("p a t d -> p (a t d)")[:, 0:SLOTS * ROW].rearrange("p (s r) -> p s r", s=SLOTS)
        xT = zT[:, 0, 0:2 * P].rearrange("p (s t) -> p s t", s=2)
        yb = y[:].rearrange("p a t d -> p (a t) d")
        cmp = headsT[:].rearrange("p a t -> p (a t)")[:, 0:NB * E].rearrange("p (b e) -> p b e", e=E)
        sel = qk0T[:].rearrange("p a t -> p (a t)")[:, 0:NB * E].rearrange("p (b e) -> p b e", e=E)
        ys_lo = vq[:].rearrange("p g t v -> p (g t v)")[:, 0:U // 2 * T * K * D].rearrange(
            "p (u t k d) -> p u t k d", u=U // 2, t=T, k=K)
        ys_hi = gate[:].rearrange("p g e t -> p (g e t)").rearrange("p (u t k d) -> p u t k d", u=U // 2, t=T, k=K)
        ys = [ys_lo[:, u] if u < U // 2 else ys_hi[:, u - U // 2] for u in range(U)]

        bank = [ctx.enter_context(nc.psum_tensor(f"bank{i}", [P, 512], F32)) for i in range(8)]
        p_turn, p_v, p_gate, p_h, p_lkv, p_route = bank[0], bank[1:3], bank[3], bank[4:6], bank[6], bank[7]
        p_po, p_wo, p_sc = p_h, p_gate, p_lkv
        p_logit = p_route[:, 0:T * E].rearrange("p (t e) -> p t e", t=T)
        p_count = p_route[:, P:P + T * K * E].rearrange("p (t k e) -> p t k e", t=T, k=K)
        p_total = p_route[:, 2 * P:2 * P + K * E].rearrange("p (k e) -> p k e", k=K)
        p_x, p_hid, p_y = bank[0:2], bank[2:4], bank[4:6]

        const_in = sem("const_in"); mod_in = sem("mod_in"); proj_in = sem("proj_in"); late_in = sem("late_in"); row_in = sem("row_in")
        x_in = [sem(f"x_in{u}") for u in range(U)]
        w1_in = sem("w1_in"); w2_in = sem("w2_in")
        zeroed = sem("zeroed"); halved = sem("halved"); padded = sem("padded"); cleared = sem("cleared")
        tri_ready = sem("tri_ready")
        c_silu = sem("c_silu"); c_spread = sem("c_spread"); mod_done = sem("mod_done"); mod_step = sem("mod_step")
        stat_step = sem("stat_step")
        var_ready = [sem(f"var_ready{i}") for i in range(4)]
        rstd_ready = [sem(f"rstd_ready{i}") for i in range(4)]
        nmr_ready = [sem(f"nmr_ready{i}") for i in range(2)]
        xn_ready = sem("xn_ready"); u_half = sem("u_half"); u_ready = sem("u_ready"); z_ready = sem("z_ready")
        z_turned = sem("z_turned"); zt_ready = sem("zt_ready")
        vq_done = sem("vq_done"); vq_biased = sem("vq_biased"); vq_ready = sem("vq_ready")
        gate_done = sem("gate_done"); gate_ready = sem("gate_ready")
        head_step = sem("head_step"); heads_ready = sem("heads_ready"); heads_turned = sem("heads_turned")
        t_ready = sem("t_ready")
        lkv_done = sem("lkv_done"); lkv_ready = sem("lkv_ready")
        scores_done = sem("scores_done"); scores_biased = sem("scores_biased"); att_ready = sem("att_ready")
        po_done = sem("po_done"); go_ready = sem("go_ready"); wo_done = sem("wo_done"); y_ready = sem("y_ready")
        yn_ready = sem("yn_ready"); x2_step = sem("x2_step"); x2_ready = sem("x2_ready")
        h2n_ready = sem("h2n_ready"); h2_half = sem("h2_half"); h2_ready = sem("h2_ready")
        h2_turned = sem("h2_turned"); h2t_ready = sem("h2t_ready")
        logits_done = sem("logits_done"); route_step = sem("route_step"); gap_ready = sem("gap_ready")
        lean_ready = sem("lean_ready"); oh_ready = sem("oh_ready"); counted = sem("counted")
        rows_ready = sem("rows_ready"); scattered = sem("scattered")
        totalled = sem("totalled"); pads_known = sem("pads_known"); pads_out = sem("pads_out")
        blocks_ready = sem("blocks_ready")
        block_in = [sem(f"block_in{k}") for k in range(SLOTS)]
        x_turned = sem("x_turned"); xT_ready = sem("xT_ready"); w1_ready = sem("w1_ready")
        hid_done = sem("hid_done"); hid_ready = sem("hid_ready"); y_done = sem("y_done")
        meta_step = sem("meta_step"); meta_ready = sem("meta_ready"); y_scaled = sem("y_scaled")
        y_out = [sem(f"y_out{k}") for k in range(SLOTS)]
        y_in = [sem(f"y_in{u}") for u in range(U)]
        taken = sem("taken"); fin_step = sem("fin_step"); fin_ready = sem("fin_ready"); stored = sem("stored")

        block = ctx.enter_context(nc.Block())

        def after(eng, s, value):
            if value > 0:
                eng.wait_ge(s, value)

        def tiles(u):
            return X[:, T * u:T * u + T, :]

        def features(u):
            return hx[:, T * u:T * u + T, 0:D]

        def blocks(eng, step):
            with eng.Fori(0, NB // SLOTS) as i:
                for k in range(SLOTS):
                    step(i * SLOTS + k, k, i)

        @block.sync
        def _(sp):
            sp.dma_start(X[:, 0:T, :], x[0]).then_inc(x_in[0], 16)
            sp.dma_start(cT[:], c_t).then_inc(mod_in, 16)
            sp.dma_start(wmod_s[:], w_mod).then_inc(mod_in, 16)
            sp.dma_start(X[:, T:2 * T, :], x[1]).then_inc(x_in[1], 16)
            sp.dma_start(row[:], rows.partition_broadcast(P)).then_inc(row_in, 16)
            sp.dma_start(con[:], consts).then_inc(const_in, 16)
            sp.dma_start(col[:], cols).then_inc(proj_in, 16)
            sp.dma_start(wvq_s[:], w_vq).then_inc(proj_in, 16)
            sp.dma_start(wg_s[:], w_g).then_inc(proj_in, 16)
            for u in range(2, U):
                sp.dma_start(tiles(u), x[u]).then_inc(x_in[u], 16)
                if u == 2:
                    sp.dma_start(wo_s[:], w_o).then_inc(late_in, 16)
                    sp.dma_start(wr_s[:], w_r).then_inc(late_in, 16)
                    sp.dma_start(bias_s[:], bias).then_inc(late_in, 16)
            sp.dma_start(w1_s[:], w_1).then_inc(w1_in, 16)
            sp.dma_start(w2_s[:], w_2).then_inc(w2_in, 16)
            sp.wait_ge(padded, 2)
            sp.dma_start(from_experts.rearrange("(p n) d -> p n d", p=P),
                         pad[:, 0:D].unsqueeze(1).to_broadcast([P, K * B * N // P, D])).then_inc(cleared, 16)
            sp.dma_start(to_experts[SPARE:SPARE + P, :], pad[:]).then_inc(pads_out, 16)
            sp.wait_ge(pads_known, 1)
            for e in range(E):
                at = sp.value_load(pad_row[0:1, e:e + 1], min_val=0, max_val=SPARE - P)
                sp.dma_start(to_experts[bass.ds(at, P), :], pad[:]).then_inc(pads_out, 16)
            sp.wait_ge(pads_out, 16 * (E + 1))
            sp.wait_ge(scattered, 16 * K * NT)
            sp.wait_ge(blocks_ready, 1)

            def load(j, k, i):
                sp.wait_ge(meta_ready, j + 1)
                sp.wait_ge(x_turned, j + 1)
                at = sp.value_load(blk_ri[0:1, bass.ds(j, 1)], min_val=0, max_val=SPARE)
                sp.dma_start(xb[:, k, :], to_experts[bass.ds(at, P), :]).then_inc(block_in[k], 16)

            blocks(sp, load)
            for k in range(SLOTS):
                sp.wait_ge(y_out[k], 16 * (NB // SLOTS))
            for u in range(U):
                src = from_experts[K * UT * u:K * UT * (u + 1), :].rearrange("(t p k) d -> p t (k d)", p=P, k=K)
                sp.dma_start(ys[u].rearrange("p t k d -> p t (k d)"), src).then_inc(y_in[u], 16)
            for u in range(U):
                sp.wait_ge(fin_ready, u + 1)
                sp.dma_start(out[u], tiles(u)).then_inc(stored, 16)
            sp.wait_ge(stored, 16 * U)

        @block.gpsimd
        def _(pool):
            for s, n in ((meta_ready, SLOTS), (x_turned, SLOTS), (xT_ready, 2), (hid_ready, 2), (hid_done, 2),
                         (y_scaled, 2), (y_done, 2)):
                pool.sem_inc(s, n)
            pool.memset(half[:], -0.5).then_inc(halved, 1)
            pool.memset(pad[:], 0.0).then_inc(padded, 1)
            pool.memset(qk0[:], 0.0).then_inc(zeroed, 1)
            pool.memset(lkv[:], 0.0).then_inc(zeroed, 1)
            pool.memset(att[:], 0.0).then_inc(zeroed, 1)
            pool.memset(ones16[:], 1.0).then_inc(zeroed, 1)
            pool.memset(before[:, 0], 0.0).then_inc(zeroed, 1)
            pool.wait_ge(halved, 1)
            pool.wait_ge(padded, 1)
            pool.memset(pad[:, D:D + 1], float(NOWHERE)).then_inc(padded, 1)

            def inverse_root(i, u):
                pool.wait_ge(var_ready[i], u + 1)
                pool.tensor_tensor(rstd[:, i, u % 2, :], var[:, i, u % 2, :], half[:], ALU.pow)\
                    .then_inc(rstd_ready[i], 1)
                if i < 2:
                    pool.wait_ge(rstd_ready[i], u + 1)
                    pool.tensor_tensor(nmr[:, i, u % 2, :], minus[:, i, u % 2, :], rstd[:, i, u % 2, :], ALU.mult)\
                        .then_inc(nmr_ready[i], 1)

            def modulate(buf, b, scale, shift, ready, step, done, u):
                pool.wait_ge(ready, u + 1)
                pool.wait_ge(mod_done, 1)
                pool.tensor_tensor(buf, buf, mod[:, b, scale:scale + 1, :].to_broadcast([P, T, D]), ALU.mult)\
                    .then_inc(step, 1)
                pool.wait_ge(step, u + 1)
                pool.tensor_tensor(buf, buf, mod[:, b, shift:shift + 1, :].to_broadcast([P, T, D]), ALU.add)\
                    .then_inc(done, 1)

            def scatter(u):
                pool.wait_ge(rows_ready, u + 1)
                for t in range(T):
                    for k in range(K):
                        pool.indirect_dma_start(
                            out=to_experts, out_offset=bass.IndirectOffsetOnAxis(ap=target[:, u, t, k:k + 1], axis=0),
                            in_=hx[:, T * u + t, :], in_offset=None, bounds_check=SPARE - 1, oob_is_err=False)\
                            .then_inc(scattered, 16)

            for step, u in order():
                b = u // UB
                if step == "stats_x":
                    inverse_root(0, u)
                elif step == "norm_x":
                    modulate(xn[:, u % 2], b, 1, 0, xn_ready, u_half, u_ready, u)
                elif step == "stats_u":
                    inverse_root(1, u)
                elif step == "scores":
                    pool.wait_ge(xn_ready, u + 1)
                    pool.wait_ge(mod_done, 2)
                    pool.tensor_tensor(tiles(u), tiles(u), ln2b[:, b:b + 1, :].to_broadcast([P, T, D]), ALU.add)\
                        .then_inc(x2_step, 1)
                elif step == "project_out":
                    inverse_root(2, u)
                elif step == "norm_y":
                    pool.wait_ge(yn_ready, u + 1)
                    pool.tensor_tensor(yn[:, u % 2], yn[:, u % 2], ln2w[:, b:b + 1, :].to_broadcast([P, T, D]),
                                       ALU.mult).then_inc(x2_step, 1)
                    pool.wait_ge(x2_step, min(UB * (b + 1), u + 3) + u + 1)
                    pool.tensor_tensor(tiles(u), tiles(u), yn[:, u % 2], ALU.add).then_inc(x2_ready, 1)
                elif step == "stats_x2":
                    inverse_root(3, u)
                elif step == "norm_x2":
                    modulate(features(u), b, 4, 3, h2n_ready, h2_half, h2_ready, u)
                elif step == "places":
                    scatter(u)

            def scatter_block(j, k, i):
                pool.wait_ge(y_scaled, j + 1 + 2)
                pool.sem_inc(taken, 1)
                pool.indirect_dma_start(
                    out=from_experts, out_offset=bass.IndirectOffsetOnAxis(ap=dest[:, k:k + 1], axis=0),
                    in_=yb[:, k, :], in_offset=None, bounds_check=K * B * N - 1, oob_is_err=False)\
                    .then_inc(y_out[k], 16)

            pool.wait_ge(cleared, 16)
            blocks(pool, scatter_block)

        @block.scalar
        def _(act):
            act.wait_ge(mod_in, 32)
            act.activation(sc[:], cT[:], ACT.Silu).then_inc(c_silu, 1)

            def normalise(i, dst, src, u, done):
                act.wait_ge(nmr_ready[i], u + 1)
                for t in range(T):
                    last = act.activation(dst[:, t, :], src[:, t, :], ACT.Identity, bias=nmr[:, i, u % 2, t:t + 1],
                                          scale=rstd[:, i, u % 2, t:t + 1])
                last.then_inc(done, 1)

            def project(u):
                act.wait_ge(z_turned, u + 1)
                after(act, gate_done, EB * (u - 1))
                act.activation(zT[:, u % 2, :], p_turn[:, :], ACT.Identity, bias=col[:, 1:2], scale=col[:, 0:1])\
                    .then_inc(zt_ready, 1)
                for e in range(EB):
                    act.wait_ge(gate_done, EB * u + e + 1)
                    after(act, go_ready, u - UB + 1)
                    act.activation(gate[:, u % UB, e, :], p_gate[:, :], ACT.Silu, bias=col[:, 2 + e:3 + e])\
                        .then_inc(gate_ready, 1)

            def turn_heads(u):
                act.wait_ge(heads_turned, u + 1)
                after(act, po_done, u - UB + 1)
                act.activation(headsT[:, u % UB, :], p_h[0][:, :], ACT.Copy)
                act.activation(qk0T[:, u % UB, :], p_h[1][:, :], ACT.Copy).then_inc(t_ready, 1)

            act.wait_ge(proj_in, 48)
            for step, u in order():
                if step == "norm_x":
                    after(act, z_ready, u - 1)
                    normalise(0, xn[:, u % 2], tiles(u), u, xn_ready)
                elif step == "norm_u":
                    after(act, z_turned, u - UB + 1)
                    normalise(1, z[:, u % UB], xn[:, u % 2], u, z_ready)
                elif step == "project":
                    project(u)
                elif step == "values":
                    act.wait_ge(vq_biased, T * (u + 1))
                    act.activation(vq[:, u % UB], vq[:, u % UB], ACT.Silu).then_inc(vq_ready, 1)
                elif step == "turn_heads":
                    turn_heads(u)
                elif step == "logits":
                    act.wait_ge(h2_turned, u + 1)
                    after(act, logits_done, u)
                    act.activation(h2T[:, :], p_turn[:, :], ACT.Copy).then_inc(h2t_ready, 1)
                elif step == "places":
                    act.wait_ge(gap_ready, u + 1)
                    act.activation(lean[:, u % 2, :], gap[:, u % 2, :], ACT.Tanh, scale=0.5).then_inc(lean_ready, 1)

            def gelu(j, k, i):
                act.wait_ge(hid_done, j + 1 + 2)
                act.wait_ge(y_done, j + 1)
                act.activation(hid[:, k % 2, :], p_hid[k % 2][:, :], ACT.Gelu).then_inc(hid_ready, 1)

            blocks(act, gelu)

        @block.vector
        def _(dve):
            dve.wait_ge(c_silu, 1)
            dve.tensor_copy(c_rep[:], sc[:, :].unsqueeze(2).to_broadcast([P, B, P])).then_inc(c_spread, 1)

            def mod_vectors():
                dve.wait_ge(row_in, 16)
                dve.wait_ge(mod_step, 4)
                for b in range(B):
                    for j in range(2):
                        last = dve.tensor_copy(
                            mod[:, b, 3 * j:3 * j + 3, :],
                            bank[1 + 3 * b + j][:, 0:3 * D].rearrange("p (k d) -> p k d", k=3))
                last.then_inc(mod_step, 1)
                dve.wait_ge(mod_step, 5)
                dve.tensor_scalar(mod[:, :, 1::3, :], mod[:, :, 1::3, :], 1.0, None, ALU.add).then_inc(mod_done, 1)
                dve.tensor_scalar(mtmp[:, :, :, 0, :], mod[:, :, 2::3, :], 0.0, 2.0, ALU.is_ge, ALU.mult)
                for b in range(B):
                    last = dve.scalar_tensor_tensor(out=mtmp[:, b, :, 1, :], in0=mod[:, b, 2::3, :], scalar=-1.0,
                                                    in1=mod[:, b, 2::3, :], op0=ALU.mult, op1=ALU.max)
                last.then_inc(mod_step, 1)
                dve.wait_ge(mod_step, 6)
                dve.tensor_scalar(mtmp[:, :, :, 1, :], mtmp[:, :, :, 1, :], 0.25, None, ALU.max).then_inc(mod_step, 1)
                dve.wait_ge(mod_step, 7)
                for b in range(B):
                    last = dve.scalar_tensor_tensor(out=mod[:, b, 2::3, :], in0=mtmp[:, b, :, 0, :], scalar=-1.0,
                                                    in1=mtmp[:, b, :, 1, :], op0=ALU.add, op1=ALU.mult)
                last.then_inc(mod_step, 1)
                dve.wait_ge(mod_step, 8)
                for vector, at in ((ln2w, R_W2), (ln2b, R_B2)):
                    last = dve.tensor_tensor(vector[:], mod[:, :, 2, :],
                                             row[:, at:at + D].unsqueeze(1).to_broadcast([P, B, D]), ALU.mult)
                last.then_inc(mod_done, 1)

            count = {"stat": 0, "route": 0}

            def then_stat(ins):
                count["stat"] += 1
                ins.then_inc(stat_step, 1)
                dve.wait_ge(stat_step, count["stat"])

            def then_route(ins):
                count["route"] += 1
                ins.then_inc(route_step, 1)
                dve.wait_ge(route_step, count["route"])

            def variance(i, src, u):
                after(dve, (xn_ready, z_ready, yn_ready, h2n_ready)[i], u - 1)
                for t in range(T):
                    last = dve.bn_stats(stats[:, i, u % 2, t, :], src[:, t, :])
                then_stat(last)
                for t in range(T):
                    last = dve.bn_aggr(mv[:, i, u % 2, t, :], stats[:, i, u % 2, t, :])
                then_stat(last)
                if i < 2:
                    dve.tensor_scalar(minus[:, i, u % 2, :], mv[:, i, u % 2, :, 0], -1.0, None, ALU.mult)
                dve.tensor_scalar(var[:, i, u % 2, :], mv[:, i, u % 2, :, 1], EPS, None, ALU.add)\
                    .then_inc(var_ready[i], 1)

            def normalise(i, dst, src, u, done):
                dve.wait_ge(rstd_ready[i], u + 1)
                for t in range(T):
                    last = dve.tensor_scalar(dst[:, t, :], src[:, t, :], mv[:, i, u % 2, t, 0:1],
                                             rstd[:, i, u % 2, t:t + 1], ALU.subtract, ALU.mult)
                last.then_inc(done, 1)

            def bias_vq(u):
                after(dve, po_done, u - UB + 1)
                for t in range(T):
                    dve.wait_ge(vq_done, T * u + t + 1)
                    dve.tensor_tensor(vq[:, u % UB, t, :], p_v[t % 2][:, 0:VQ], row[:, R_VQ:R_VQ + VQ], ALU.add)\
                        .then_inc(vq_biased, 1)

            def make_heads(u):
                g = u % UB
                n = 3 * u
                full = [P, T, NH, QK]
                qk = vq[:, g, :, H:VQ].unsqueeze(2).to_broadcast(full)
                gam = row[:, R_GAM:R_GAM + P].rearrange("p (h d) -> p h d", h=NH).unsqueeze(1).to_broadcast(full)
                bet = row[:, R_BET:R_BET + P].rearrange("p (h d) -> p h d", h=NH).unsqueeze(1).to_broadcast(full)
                cs = cos[:, T * g:T * g + T, :].unsqueeze(2).to_broadcast(full)
                sn = sin[:, T * g:T * g + T, :].unsqueeze(2).to_broadcast(full)
                R = QK // 2
                dve.wait_ge(vq_ready, u + 1)
                dve.tensor_tensor(hA[:], qk, gam, ALU.mult).then_inc(head_step, 1)
                dve.wait_ge(head_step, n + 1)
                dve.tensor_tensor(hA[:], hA[:], bet, ALU.add).then_inc(head_step, 1)
                dve.wait_ge(head_step, n + 2)
                dve.tensor_tensor(hB[:], hA[:], cs, ALU.mult)
                dve.tensor_tensor(hC[:, :, :, 0:R], hA[:, :, :, R:QK], sn[:, :, :, 0:R], ALU.mult)
                dve.tensor_tensor(hC[:, :, :, R:QK], hA[:, :, :, 0:R], sn[:, :, :, R:QK], ALU.mult)\
                    .then_inc(head_step, 1)
                dve.wait_ge(head_step, n + 3)
                after(dve, lkv_done, u - 1)
                dve.tensor_tensor(qk0[:, u % 2, :, 0:QK], hB[:, :, 2, :], hC[:, :, 2, :], ALU.add)
                dve.tensor_tensor(heads[:, u % 2], hB[:], hC[:], ALU.add).then_inc(heads_ready, 1)
                dve.wait_ge(heads_ready, u + 1)

            def square_relu(u):
                dve.wait_ge(scores_done, u + 1)
                after(dve, att_ready, u)
                after(dve, po_done, u - 1)
                for a in range(2):
                    last = dve.scalar_tensor_tensor(
                        out=att1[G * a:G * a + G], scalar=1.0 / G,
                        in0=p_sc[G * a:G * a + G, :].rearrange("p (t i) -> p t i", t=T)[:, :, G * a:G * a + G],
                        in1=bias_s[G * a:G * a + G, :].unsqueeze(1).to_broadcast([G, T, G]),
                        op0=ALU.mult, op1=ALU.add)
                last.then_inc(scores_biased, 1)
                dve.wait_ge(scores_biased, u + 1)
                for a in range(2):
                    last = dve.scalar_tensor_tensor(
                        out=att[G * a:G * a + G, u % 2, :, G * a:G * a + G], in0=att1[G * a:G * a + G], scalar=0.0,
                        in1=att1[G * a:G * a + G], op0=ALU.max, op1=ALU.mult)
                last.then_inc(att_ready, 1)

            def gated(u):
                dve.wait_ge(po_done, u + 1)
                dve.wait_ge(gate_ready, EB * (u + 1))
                after(dve, wo_done, u - 1)
                for e in range(EB):
                    last = dve.tensor_tensor(go[:, u % 2, e, :], p_po[e][:, :], gate[:, u % UB, e, :], ALU.mult)
                last.then_inc(go_ready, 1)

            def bias_out(u):
                dve.wait_ge(wo_done, u + 1)
                after(dve, yn_ready, u - 1)
                dve.tensor_tensor(y[:, u % 2], p_wo[:, :].rearrange("p (t d) -> p t d", t=T),
                                  row[:, R_BO:R_BO + D].unsqueeze(1).to_broadcast([P, T, D]), ALU.add)\
                    .then_inc(y_ready, 1)
                dve.wait_ge(y_ready, u + 1)
                variance(2, y[:, u % 2], u)

            def choose(u):
                s = u % 2
                dve.wait_ge(logits_done, u + 1)
                after(dve, rows_ready, u - 1)
                for t in range(T):
                    last = dve.max(top[:, s, t, :], p_logit[:, t, :])
                then_route(last)
                for t in range(T):
                    last = dve.max_index(top_i[:, s, t, :], top[:, s, t, :], p_logit[:, t, :])
                dve.tensor_tensor(gap[:, s, :], top[:, s, :, 1], top[:, s, :, 0], ALU.subtract).then_inc(gap_ready, 1)
                dve.wait_ge(gap_ready, u + 1)
                then_route(dve.tensor_copy(first_e[:, s], top_i[:, s, :, 0:K]))
                dve.tensor_tensor(oh[:, s], expert_no.unsqueeze(1).unsqueeze(1).to_broadcast([P, T, K, E]),
                                  first_e[:, s].unsqueeze(3).to_broadcast([P, T, K, E]), ALU.is_equal)\
                    .then_inc(route_step, 1)
                count["route"] += 1
                dve.wait_ge(route_step, count["route"])
                for t in range(T):
                    n = T * u + t
                    ins = dve.tensor_tensor(before[:, n + 1], before[:, n], oh[:, s, t], ALU.add)
                    if t < T - 1:
                        then_route(ins)
                ins.then_inc(oh_ready, 1)

            def rows_of(u):
                s = u % 2
                dve.wait_ge(counted, u + 1)
                then_route(dve.tensor_tensor(picked[:], p_count, oh[:, s], ALU.mult))
                then_route(dve.tensor_reduce(place[:], picked[:], AX.X, ALU.add))
                dve.tensor_scalar(far[:], place[:], float(CAP), float(NOWHERE), ALU.is_gt, ALU.mult)
                dve.tensor_scalar(side[:, :, 0], place[:, :, 0], -1.0, None, ALU.add)
                dve.tensor_scalar(side[:, :, 1], place[:, :, 1], -1.0, None, ALU.mult)
                then_route(dve.tensor_scalar(base[:], first_e[:, s], float(PITCH), float(CAP), ALU.mult, ALU.add))
                then_route(dve.tensor_tensor(base[:], base[:], side[:], ALU.add))
                dve.tensor_tensor(target[:, u], base[:], far[:], ALU.add)
                mark = hx[:, T * u:T * u + T, D:ROW]
                dve.wait_ge(lean_ready, u + 1)
                dve.tensor_copy(mark[:, :, 0], token_mark[:, T * u:T * u + T])
                dve.tensor_scalar(mark[:, :, 1], lean[:, s, :], 0.5, 0.5, ALU.mult, ALU.add)
                dve.tensor_scalar(mark[:, :, 2], lean[:, s, :], -1.0, None, ALU.mult)
                dve.tensor_copy(mark[:, :, 3], first_e[:, s, :, 0]).then_inc(rows_ready, 1)

            dve.wait_ge(x_in[0], 16)

            for step, u in order():
                if step == "stats_x":
                    dve.wait_ge(x_in[u], 16)
                    variance(0, tiles(u), u)
                    if u == 0:
                        mod_vectors()
                        dve.wait_ge(const_in, 16)
                        dve.tensor_copy(tri16[:], con[:, C_TRI:C_TRI + P]).then_inc(tri_ready, 1)
                        dve.wait_ge(zeroed, 5)
                elif step == "stats_u":
                    dve.wait_ge(u_ready, u + 1)
                    variance(1, xn[:, u % 2], u)
                elif step == "heads":
                    make_heads(u)
                elif step == "values":
                    bias_vq(u)
                elif step == "linear":
                    dve.wait_ge(lkv_done, UB * (u + 1))
                    dve.tensor_scalar(lkv[QK:2 * QK, u, :], p_lkv[QK:2 * QK, 0:H], 1.0 / N, None, ALU.mult)\
                        .then_inc(lkv_ready, 1)
                elif step == "scores":
                    square_relu(u)
                elif step == "attend":
                    gated(u)
                elif step == "project_out":
                    bias_out(u)
                elif step == "norm_y":
                    after(dve, x2_ready, u - 1)
                    normalise(2, yn[:, u % 2], y[:, u % 2], u, yn_ready)
                elif step == "stats_x2":
                    dve.wait_ge(x2_ready, u + 1)
                    variance(3, tiles(u), u)
                elif step == "norm_x2":
                    normalise(3, features(u), tiles(u), u, h2n_ready)
                elif step == "logits":
                    choose(u)
                elif step == "places":
                    rows_of(u)

            dve.wait_ge(totalled, 1)
            then_route(dve.tensor_scalar(cnt[:], p_total, float(CAP), None, ALU.min))
            dve.memset(one_e[:], 1.0)
            dve.tensor_tensor(pad_row[:], expert_row, cnt[:, 0], ALU.add).then_inc(pads_known, 1)
            then_route(dve.tensor_tensor(cnt_all[:], cnt[:, 0], cnt[:, 1], ALU.add))
            then_route(dve.tensor_scalar(cnt_i[:], cnt_all[:], float(P - 1), None, ALU.add))
            then_route(dve.tensor_scalar(cnt_i[:], cnt_i[:], P.bit_length() - 1, None, ALU.logical_shift_right))
            then_route(dve.tensor_copy(cnt_all[:], cnt_i[:]))
            then_route(dve.tensor_tensor_scan(ends[:], one_e[:], cnt_all[:], 0.0, ALU.mult, ALU.add))
            then_route(dve.tensor_tensor(start_row[:], cnt_all[:], ends[:], ALU.subtract))
            then_route(dve.scalar_tensor_tensor(out=start_row[:], in0=start_row[:], scalar=float(P),
                                                in1=expert_row, op0=ALU.mult, op1=ALU.add))
            then_route(dve.tensor_tensor(start_row[:], start_row[:], cnt[:, 1], ALU.subtract))
            then_route(dve.tensor_scalar(blk_r[:], block_row, float(SPARE), 1.0 / P, ALU.add, ALU.mult))
            then_route(dve.tensor_tensor(cmp, ends[:].unsqueeze(1).to_broadcast([P, NB, E]),
                                         blk_r[:].unsqueeze(2).to_broadcast([P, NB, E]), ALU.is_le))
            then_route(dve.tensor_reduce(blk_e[:], cmp, AX.X, ALU.add))
            then_route(dve.tensor_tensor(sel, expert_no.unsqueeze(1).to_broadcast([P, NB, E]),
                                         blk_e[:].unsqueeze(2).to_broadcast([P, NB, E]), ALU.is_equal))
            then_route(dve.tensor_tensor(sel, sel, start_row[:].unsqueeze(1).to_broadcast([P, NB, E]), ALU.mult))
            dve.tensor_scalar(blk_ei[:], blk_e[:], float(E - 1), None, ALU.min)
            then_route(dve.tensor_reduce(blk_r[:], sel, AX.X, ALU.add))
            then_route(dve.scalar_tensor_tensor(out=cmp[:, :, 0], in0=blk_e[:], scalar=float(E), in1=block_row,
                                                op0=ALU.is_lt, op1=ALU.mult))
            then_route(dve.tensor_tensor(blk_r[:], blk_r[:], cmp[:, :, 0], ALU.add))
            dve.tensor_scalar(blk_ri[:], blk_r[:], float(SPARE), None, ALU.add).then_inc(blocks_ready, 1)
            dve.wait_ge(blocks_ready, 1)
            dve.wait_ge(w1_in, 16)

            regs = [dve.alloc_register(f"expert_of{k}") for k in range(SLOTS)]

            def expert_front(j, k):
                e = dve.snap(regs[k], min_val=0, max_val=E - 1)
                dve.wait_ge(hid_done, j + 1)
                dve.tensor_copy(w1_b[:, k % 2, :], w1_s[:, bass.ds(e, 1), :].rearrange("p e f -> p (e f)"))\
                    .then_inc(w1_ready, 1)
                dve.wait_ge(x_turned, j + 1 + SLOTS)
                dve.tensor_copy(xT[:, k % 2, :], p_x[k % 2][:, 0:P]).then_inc(xT_ready, 1)

            def meta(j, k, i, first=False):
                dve.wait_ge(block_in[k], 16 * i + 16)
                if not first:
                    dve.wait_ge(y_out[k], 16 * i)
                dve.tensor_tensor(is_first[:, k:k + 1], xb[:, k, D + 3:D + 4], blk_e[:, bass.ds(j, 1)],
                                  ALU.is_equal).then_inc(meta_step, 1)
                dve.wait_ge(meta_step, j + 1)
                dve.scalar_tensor_tensor(out=weight[:, k:k + 1], in0=is_first[:, k:k + 1],
                                         scalar=xb[:, k, D + 2:D + 3], in1=xb[:, k, D + 1:D + 2],
                                         op0=ALU.mult, op1=ALU.add)
                dve.tensor_tensor(dest[:, k:k + 1], xb[:, k, D:D + 1], is_first[:, k:k + 1], ALU.subtract)\
                    .then_inc(meta_ready, 1)
                dve.wait_ge(meta_ready, j + 1 + SLOTS)

            def scale_out(j, k):
                dve.wait_ge(y_done, j + 1 + 2)
                dve.tensor_scalar(yb[:, k, :], p_y[k % 2][:, 0:D], weight[:, k:k + 1], None, ALU.mult)\
                    .then_inc(y_scaled, 1)

            dve.load(regs, blk_ei[0:1, 0:SLOTS])
            for k in range(2):
                expert_front(k, k)
            def group(i, first=False):
                dve.load(regs, blk_ei[0:1, 2:2 + SLOTS] if first else blk_ei[0:1, bass.ds(i * SLOTS + 2, SLOTS)])
                for k in range(SLOTS):
                    j = i * SLOTS + k
                    expert_front(j + 2, k)
                    meta(j, k, i, first)
                    scale_out(j, k)

            group(0, first=True)
            with dve.Fori(1, NB // SLOTS - 1) as i:
                group(i)
            dve.load(regs, blk_ei[0:1, NB - SLOTS:NB])
            for k in range(SLOTS):
                j = NB - SLOTS + k
                if k + 2 < SLOTS:
                    expert_front(j + 2, k + 2)
                meta(j, k, NB // SLOTS - 1)
                scale_out(j, k)

            for u in range(U):
                dve.wait_ge(y_in[u], 16)
                dve.tensor_tensor(ys[u][:, :, 0, :], ys[u][:, :, 0, :], ys[u][:, :, 1, :], ALU.add).then_inc(fin_step, 1)
                dve.wait_ge(fin_step, 2 * u + 1)
                dve.tensor_tensor(ys[u][:, :, 0, :], ys[u][:, :, 0, :],
                                  mod[:, u // UB, 5:6, :].to_broadcast([P, T, D]), ALU.mult).then_inc(fin_step, 1)
                dve.wait_ge(fin_step, 2 * u + 2)
                dve.tensor_tensor(tiles(u), tiles(u), ys[u][:, :, 0, :], ALU.add).then_inc(fin_ready, 1)

        @block.tensor
        def _(pe):
            pe.wait_ge(c_spread, 1)
            pe.wait_ge(mod_in, 32)
            for b in range(B):
                for j in range(2):
                    pe.matmul(bank[1 + 3 * b + j][:, 0:3 * D], c_rep[:, b, :], wmod_s[:, 3 * D * j:3 * D * (j + 1)],
                              start=True, stop=True).then_inc(mod_step, 1)
            pe.wait_ge(const_in, 16)
            pe.wait_ge(proj_in, 48)
            pe.wait_ge(mod_step, 5)
            n = dict.fromkeys(("project", "turn_heads", "scores", "attend", "project_out", "logits"), 0)

            def project(u):
                pe.wait_ge(z_ready, u + 1)
                after(pe, zt_ready, u)
                after(pe, h2t_ready, n["logits"])
                for t in range(T):
                    last = pe.transpose(p_turn[:, P * t:P * t + P], z[:, u % UB, t, :], ident)
                last.then_inc(z_turned, 1)
                pe.wait_ge(zt_ready, u + 1)
                after(pe, y_ready, n["project_out"])
                for e in range(EB):
                    after(pe, gate_ready, EB * u + e)
                    pe.matmul(p_gate[:, :], wg_s[:, P * e:P * e + P], zT[:, u % 2, :], start=True, stop=True)\
                        .then_inc(gate_done, 1)
                    for t in range(2 * e, 2 * e + 2):
                        after(pe, vq_biased, T * u + t - 1)
                        pe.matmul(p_v[t % 2][:, 0:VQ], zT[:, u % 2, P * t:P * t + P], wvq_s[:], start=True, stop=True)\
                            .then_inc(vq_done, 1)

            def turn_heads(u):
                pe.wait_ge(heads_ready, u + 1)
                after(pe, t_ready, u)
                after(pe, go_ready, n["attend"])
                after(pe, scores_biased, n["scores"])
                for t in range(T):
                    pe.transpose(p_h[0][:, P * t:P * t + P], heads[:, u % 2, t].rearrange("p h d -> p (h d)"), ident)
                    last = pe.transpose(p_h[1][:, P * t:P * t + P], qk0[:, u % 2, t, :], ident)
                last.then_inc(heads_turned, 1)
                for t in range(T):
                    last = pe.matmul(p_lkv[QK:2 * QK, 0:H], heads[:, u % 2, t, 3, :], vq[:, u % UB, t, 0:H],
                                     start=(u % UB == 0 and t == 0), stop=(u % UB == UB - 1 and t == T - 1))
                last.then_inc(lkv_done, 1)

            def scores(u):
                pe.wait_ge(t_ready, u + 1)
                pe.wait_ge(late_in, 48)
                pe.wait_ge(lkv_ready, u // UB + 1)
                after(pe, scores_biased, u)
                for t in range(T):
                    last = pe.matmul(p_sc[:, P * t:P * t + P], qk0T[:, u % UB, P * t:P * t + P],
                                     headsT[:, u % UB, P * t:P * t + P], start=True, stop=True)
                last.then_inc(scores_done, 1)

            def attend(u):
                b = u // UB
                pe.wait_ge(t_ready, n["turn_heads"])
                after(pe, go_ready, u)
                pe.wait_ge(att_ready, u + 1)
                for e in range(EB):
                    for t in range(T):
                        tile = p_po[e][:, P * t:P * t + P]
                        pe.matmul(tile, lkv[:, b, P * e:P * e + P], headsT[:, u % UB, P * t:P * t + P],
                                  start=True, stop=False)
                        last = pe.matmul(tile, vq[:, u % UB, t, P * e:P * e + P], att[:, u % 2, t, :],
                                         start=False, stop=True)
                last.then_inc(po_done, 1)

            def project_out(u):
                pe.wait_ge(go_ready, u + 1)
                after(pe, gate_ready, EB * n["project"])
                after(pe, y_ready, u)
                for t in range(T):
                    for e in range(EB):
                        last = pe.matmul(p_wo[:, P * t:P * t + P], go[:, u % 2, e, P * t:P * t + P], wo_s[:, e, :],
                                         start=(e == 0), stop=(e == EB - 1))
                last.then_inc(wo_done, 1)

            def logits(u):
                pe.wait_ge(h2_ready, u + 1)
                after(pe, zt_ready, n["project"])
                after(pe, h2t_ready, u)
                for t in range(T):
                    last = pe.transpose(p_turn[:, P * t:P * t + P], hx[:, T * u + t, 0:D], ident)
                last.then_inc(h2_turned, 1)
                pe.wait_ge(h2t_ready, u + 1)
                after(pe, rows_ready, u)
                for t in range(T):
                    last = pe.matmul(p_logit[:, t, :], h2T[:, P * t:P * t + P], wr_s[:], start=True, stop=True)
                last.then_inc(logits_done, 1)

            def places(u):
                pe.wait_ge(oh_ready, u + 1)
                pe.wait_ge(tri_ready, 1)
                flat = p_route[:, P:P + T * K * E]
                pe.matmul(flat, ones16[:], before[:, T * u:T * u + T].rearrange("p t k e -> p (t k e)"),
                          start=True, stop=False)
                pe.matmul(flat, tri16[:], oh[:, u % 2].rearrange("p t k e -> p (t k e)"),
                          start=False, stop=True).then_inc(counted, 1)

            for step, u in order():
                if step == "project":
                    project(u)
                elif step == "turn_heads":
                    turn_heads(u)
                elif step == "scores":
                    scores(u)
                elif step == "attend":
                    attend(u)
                elif step == "project_out":
                    project_out(u)
                elif step == "logits":
                    logits(u)
                elif step == "places":
                    places(u)
                if step in n:
                    n[step] += 1
            pe.wait_ge(rows_ready, U)
            pe.matmul(p_route[:, 2 * P:2 * P + K * E], ones16[:], before[:, NT].rearrange("p k e -> p (k e)"),
                      start=True, stop=True).then_inc(totalled, 1)

            pe.wait_ge(w2_in, 16)
            pe.wait_ge(blocks_ready, 1)
            regs = [pe.alloc_register(f"expert_of{k}") for k in range(SLOTS)]

            def turn_x(j, k, loads):
                pe.wait_ge(block_in[k], 16 * loads)
                pe.wait_ge(xT_ready, j + 1)
                pe.transpose(p_x[k % 2][:, 0:P], xb[:, k, 0:D], ident).then_inc(x_turned, 1)

            def first_layer(j, k):
                pe.wait_ge(xT_ready, j + 1 + 2)
                pe.wait_ge(w1_ready, j + 1)
                pe.wait_ge(hid_ready, j + 1)
                for f in range(FB):
                    last = pe.matmul(p_hid[k % 2][:, P * f:P * f + P], w1_b[:, k % 2, P * f:P * f + P], xT[:, k % 2, :],
                                     start=True, stop=True)
                last.then_inc(hid_done, 1)

            def second_layer(j, k, e):
                pe.wait_ge(hid_ready, j + 1 + 2)
                pe.wait_ge(y_scaled, j + 1)
                for f in range(FB):
                    last = pe.matmul(p_y[k % 2][:, 0:D], hid[:, k % 2, P * f:P * f + P],
                                     w2_s[:, bass.ds(e, 1), f, :].rearrange("p e d -> p (e d)"),
                                     start=(f == 0), stop=(f == FB - 1))
                last.then_inc(y_done, 1)

            turn_x(0, 0, 1)
            first_layer(0, 0)
            turn_x(1, 1, 1)
            with pe.Fori(0, NB // SLOTS - 1) as i:
                pe.load(regs, blk_ei[0:1, bass.ts(i, SLOTS)])
                for k in range(SLOTS):
                    j = i * SLOTS + k
                    e = pe.snap(regs[k], min_val=0, max_val=E - 1)
                    first_layer(j + 1, (k + 1) % SLOTS)
                    turn_x(j + 2, (k + 2) % SLOTS, i + 1 + (k + 2) // SLOTS)
                    second_layer(j, k, e)
            pe.load(regs, blk_ei[0:1, NB - SLOTS:NB])
            for k in range(SLOTS):
                j = NB - SLOTS + k
                e = pe.snap(regs[k], min_val=0, max_val=E - 1)
                if k + 1 < SLOTS:
                    first_layer(j + 1, k + 1)
                if k + 2 < SLOTS:
                    turn_x(j + 2, k + 2, NB // SLOTS)
                second_layer(j, k, e)


def kernel(**inputs):
    import numpy as np
    import concourse.bacc as bacc
    from concourse import mybir as mb
    from concourse.bass_utils import run_bass_kernel_spmd

    a = {k: np.asarray(v) for k, v in inputs.items()}

    def at(name):
        return a["L0_attn_" + name]

    half = QK // 2
    freq = (np.float32(10000.0) ** (-np.arange(half, dtype=np.float32) / np.float32(half))).astype(np.float32)
    ang = np.arange(N, dtype=np.float32)[:, None] * freq[None, :]
    cos = np.concatenate([np.cos(ang), np.cos(ang)], 1).reshape(N // P, P, QK).transpose(1, 0, 2).reshape(P, -1)
    sin = np.concatenate([-np.sin(ang), np.sin(ang)], 1).reshape(N // P, P, QK).transpose(1, 0, 2).reshape(P, -1)
    token = np.arange(NT)[None, :] * P + np.arange(P)[:, None]
    consts = np.concatenate([np.eye(P), np.triu(np.ones((P, P))), cos, sin, np.tile(np.arange(E), (P, 1)),
                             2 * token + 1, np.tile(np.arange(NB) * P - SPARE, (P, 1)),
                             np.tile(np.arange(E) * PITCH + CAP, (P, 1))], 1).astype(np.float32)
    rows = np.concatenate([at("bv"), at("bqk"), at("gamma").ravel(), at("beta").ravel(), at("bo"),
                           at("ln2_w"), at("ln2_b")])
    cols = np.stack([at("ln1_w"), at("ln1_b"), at("bg")[:P], at("bg")[P:]], 1)
    i = np.arange(G)
    bias = at("pos_emb")[np.minimum(np.abs(i[:, None] - i[None, :]), at("pos_emb").shape[0] // 2)]
    arrays = {
        "x": at("x").reshape(U, T, P, D).transpose(0, 2, 1, 3),
        "consts": consts,
        "rows": rows,
        "cols": cols,
        "bias": np.concatenate([bias, bias], 0),
        "c_t": a["L0_c"].T,
        "w_mod": a["L0_wmod"],
        "w_vq": np.concatenate([at("Wv").T, at("Wqk").T], 1),
        "w_g": at("Wg").T,
        "w_o": at("Wo").T.reshape(EB, P, D).transpose(1, 0, 2),
        "w_r": a["L0_ffn_router_w"].T,
        "w_1": a["L0_ffn_w1"].transpose(1, 0, 2),
        "w_2": a["L0_ffn_w2"].reshape(E, FB, P, D).transpose(2, 0, 1, 3),
    }
    arrays = {k: np.ascontiguousarray(v) for k, v in arrays.items()}
    nc = bacc.Bacc("TRN2", target_bir_lowering=False, num_devices=1)
    args = [nc.dram_tensor(k, v.shape, mb.dt.from_np(v.dtype), kind="ExternalInput").ap() for k, v in arrays.items()]
    out = nc.dram_tensor("out", (U, P, T, D), mb.dt.float32, kind="ExternalOutput").ap()
    build(nc, *args, out)
    r = run_bass_kernel_spmd(nc, [arrays], core_ids=[0])
    return r.results[0]["out"].reshape(U, P, T, D).transpose(0, 2, 1, 3).reshape(B, N, D)
```

```python
from contextlib import ExitStack

import concourse.bass as bass
from concourse import mybir

F32 = mybir.dt.float32
BF16 = mybir.dt.bfloat16
I32 = mybir.dt.int32
U32 = mybir.dt.uint32
ALU = mybir.AluOpType
ACT = mybir.ActivationFunctionType
AX = mybir.AxisListType

P = 128
B, N, D = 2, 2048, 128
QK, H = 32, 256
G = 64
NH = 4
E, F, K = 8, 512, 2
T = 4
UT = T * P
UB = N // UT
U = B * UB
NT = B * N // P
CAP = int(1.25 * B * N / E * K)
EB = H // P
FB = F // P
EPS = 1e-5

PITCH = 2 * CAP + P
SPARE = E * PITCH
SLOTS = 8
NB = (K * B * N + E * (P - 1)) // P
GROUPS = NB // SLOTS
LAST = NB - SLOTS
ROW = D + 4
NOWHERE = 1 << 20

C_ID, C_TRI, C_EXP = 0, P, 2 * P
C_TOK = C_EXP + E
C_BLK = C_TOK + NT
C_BASE = C_BLK + NB
C_LEN = C_BASE + E
R_BV, R_BO, R_W2, R_B2 = 0, H, H + D, H + 2 * D
R_LEN = H + 3 * D
L_W, L_B, L_BG, L_BQ, L_GAM, L_BET, L_LEN = 0, 1, 2, 4, 6, 8, 10


def order():
    for name in SCHEDULE.split():
        step, u = name.split(".")
        yield step, int(u)


SCHEDULE = """
stats_x.0 stats_x.1 root_x.0 root_x.1 norm_x.0 mod_gates.0 modulate_x.0 norm_x.1 modulate_x.1 stats_u.0
shift_x.0 stats_x.2 root_u.0 stats_u.1 shift_x.1 norm_u.0 stats_x.3 root_u.1 turn_z.0 root_x.2 z_columns.0
norm_u.1 project_qk.0 root_x.3 norm_x.2 turn_z.1 project_a.0 silu_qk.0 stats_x.4 modulate_x.2 bias_a.0 shift_x.2
gate_a.0 rotate.0 z_columns.1 project_b.0 root_x.4 norm_x.3 stats_u.2 turn_lin_k.0 gate_b.0 modulate_x.3
project_qk.1 lin_k.0 bias_b.0 quad_k.0 stats_x.5 silu_v.0 scores.0 silu_qk.1 root_u.2 stats_u.3 project_a.1
root_x.5 square.0 root_u.3 gate_a.1 norm_u.2 bias_a.1 project_b.1 shift_x.3 rotate.1 norm_u.3 lin_kv.0 turn_z.2
sum_lkv.0 bias_b.1 quad_k.1 turn_lin_k.1 gate_b.1 lin_k.1 z_columns.2 scores.1 silu_v.1 project_qk.2 square.1
norm_x.4 lin_kv.1 turn_z.3 silu_qk.2 sum_lkv.1 modulate_x.4 stats_x.6 project_a.2 bias_a.2 shift_x.4 gate_a.2
stats_u.4 z_columns.3 project_b.2 root_x.6 norm_x.5 rotate.2 root_u.4 project_qk.3 gate_b.2 modulate_x.5
norm_u.4 bias_b.2 turn_lin_k.2 stats_x.7 project_a.3 silu_qk.3 shift_x.5 stats_u.5 turn_z.4 root_x.7 bias_a.3
gate_a.3 rotate.3 root_u.5 silu_v.2 project_b.3 z_columns.4 lin_k.2 quad_k.2 turn_lin_k.3 bias_b.3 gate_b.3
lin_k.3 silu_v.3 lin_kv.2 sum_lkv.2 quad_k.3 lin_kv.3 sum_lkv.3 norm_u.5 attend.0 norm_x.6 modulate_x.6 norm_x.7
turn_z.5 gated.0 scores.2 z_columns.5 shift_x.6 project_out.0 stats_u.6 modulate_x.7 square.2 project_qk.4
bias_y.0 root_u.6 silu_qk.4 shift_x.7 stats_u.7 project_a.4 root_y.0 norm_u.6 rotate.4 attend.1 root_u.7
norm_y.0 bias_a.4 quad_k.4 weigh_y.0 gate_a.4 add_y.0 norm_u.7 turn_lin_k.4 gated.1 project_b.4 lin_k.4
stats_x2.0 scores.3 gate_b.4 bias_b.4 root_x2.0 project_out.1 square.3 silu_v.4 norm_x2.0 lin_kv.4 bias_y.1
attend.2 scale_h.0 root_y.1 sum_lkv.4 shift_h.0 norm_y.1 turn_z.6 gated.2 scores.4 z_columns.6 weigh_y.1
project_out.2 square.4 turn_h.0 add_y.1 project_qk.5 bias_y.2 h_columns.0 logits.0 silu_qk.5 choose.0 root_y.2
project_a.5 stats_x2.1 places.0 lean.0 project_qk.6 norm_y.2 rotate.5 root_x2.1 gate_a.5 silu_qk.6 project_b.5
rows.0 turn_lin_k.5 bias_a.5 scatter_a.0 turn_z.7 norm_x2.1 weigh_y.2 attend.3 bias_b.5 add_y.2 lin_k.5 quad_k.5
scale_h.1 gate_b.5 rotate.6 silu_v.5 z_columns.7 scatter_b.0 lin_kv.5 project_a.6 gated.3 quad_k.6 stats_x2.2
project_qk.7 gate_a.6 bias_a.6 root_x2.2 shift_h.1 project_out.3 silu_qk.7 sum_lkv.5 turn_lin_k.6 bias_y.3
turn_h.1 lin_k.6 norm_x2.2 scores.5 rotate.7 root_y.3 project_b.6 h_columns.1 norm_y.3 logits.1 scale_h.2
choose.1 gate_b.6 quad_k.7 project_a.7 bias_b.6 lean.1 square.5 silu_v.6 places.1 gate_a.7 rows.1 lin_kv.6
project_b.7 bias_a.7 scatter_a.1 sum_lkv.6 gate_b.7 bias_b.7 turn_lin_k.7 shift_h.2 lin_k.7 silu_v.7 weigh_y.3
turn_h.2 add_y.3 lin_kv.7 h_columns.2 sum_lkv.7 logits.2 stats_x2.3 attend.4 scatter_b.1 choose.2 lean.2
root_x2.3 places.2 gated.4 scores.6 norm_x2.3 rows.2 project_out.4 scale_h.3 scatter_a.2 attend.5 bias_y.4
shift_h.3 square.6 root_y.4 turn_h.3 gated.5 scatter_b.2 scores.7 h_columns.3 norm_y.4 logits.3 square.7
project_out.5 weigh_y.4 attend.6 bias_y.5 add_y.4 root_y.5 choose.3 norm_y.5 gated.6 places.3 lean.3 stats_x2.4
project_out.6 rows.3 root_x2.4 attend.7 norm_x2.4 bias_y.6 scatter_a.3 scale_h.4 weigh_y.5 shift_h.4 add_y.5
turn_h.4 root_y.6 gated.7 h_columns.4 scatter_b.3 logits.4 norm_y.6 choose.4 project_out.7 weigh_y.6 lean.4
stats_x2.5 places.4 rows.4 root_x2.5 norm_x2.5 bias_y.7 scatter_a.4 scale_h.5 add_y.6 shift_h.5 stats_x2.6
turn_h.5 root_y.7 h_columns.5 scatter_b.4 logits.5 norm_y.7 choose.5 weigh_y.7 lean.5 places.5 rows.5 root_x2.6
add_y.7 stats_x2.7 scatter_a.5 norm_x2.6 scale_h.6 shift_h.6 turn_h.6 h_columns.6 root_x2.7 logits.6 choose.6
scatter_b.5 norm_x2.7 places.6 lean.6 scale_h.7 rows.6 shift_h.7 scatter_a.6 turn_h.7 h_columns.7 logits.7
choose.7 lean.7 places.7 scatter_b.6 rows.7 scatter_a.7 scatter_b.7
"""


def build(nc, x, consts, rows, cols, bias, c_t, w_mod, turns, w_v, w_qk, w_g, w_o, w_r, w_1, w_2, out):
    with ExitStack() as ctx:
        def sb(name, shape, dt=F32):
            return ctx.enter_context(nc.sbuf_tensor(name, shape, dt))

        def sem(name):
            return ctx.enter_context(nc.semaphore(name))

        to_experts = nc.dram_tensor("to_experts", (SPARE + P, ROW), F32, kind="Internal").ap()
        from_experts = nc.dram_tensor("from_experts", (K * B * N, D), F32, kind="Internal").ap()

        X = sb("X", [P, NT, D])
        con = sb("con", [P, C_LEN])
        ident = con[:, C_ID:C_ID + P]
        expert_no = con[:, C_EXP:C_TOK]
        token_mark = con[:, C_TOK:C_BLK]
        block_row = con[:, C_BLK:C_BASE]
        expert_row = con[:, C_BASE:C_LEN]
        row = sb("row", [P, R_LEN])
        col = sb("col", [P, L_LEN])
        turn = sb("turn", [P, 2, N])
        bias_s = sb("bias_s", [P, G])
        cT = sb("cT", [P, B])
        wmod_s = sb("wmod_s", [P, 6 * D])
        wv_s = sb("wv_s", [P, H])
        wqk_s = sb("wqk_s", [P, 2, P])
        wg_s = sb("wg_s", [P, H])
        wo_s = sb("wo_s", [P, EB, D])
        wr_s = sb("wr_s", [P, E])
        w1_s = sb("w1_s", [P, E, F])
        w2_s = sb("w2_s", [P, E, FB, D])
        tri16 = sb("tri16", [P, P], BF16)
        ones16 = sb("ones16", [P, P], BF16)
        half = sb("half", [P, T])
        pad = sb("pad", [P, ROW])
        sc = sb("sc", [P, B])
        c_rep = sb("c_rep", [P, B, P])
        mod = sb("mod", [P, B, 6, D])
        ln2w = sb("ln2w", [P, B, D])
        ln2b = sb("ln2b", [P, B, D])
        stats = sb("stats", [P, 4, 2, T, 6])
        mv = sb("mv", [P, 4, 2, T, 2])
        var = sb("var", [P, 4, 2, T])
        rstd = sb("rstd", [P, 4, 2, T])
        minus = sb("minus", [P, 4, 2, T])
        nmr = sb("nmr", [P, 4, 2, T])
        xn = sb("xn", [P, 2, T, D])
        z = sb("z", [P, 2, T, D])
        zT = sb("zT", [P, 2, UT])
        v = sb("v", [P, UB, T, H])
        gate = sb("gate", [P, UB, EB, UT])
        qa = sb("qa", [P, 2, UT])
        qb = sb("qb", [P, 2, UT])
        lin_k = sb("lin_k", [P, 2, T, QK])
        headsT = sb("headsT", [P, UB, UT])
        qk0T = sb("qk0T", [P, UB, UT])
        lkv = sb("lkv", [P, B, H])
        att1 = sb("att1", [P, T, G])
        att = sb("att", [P, 2, T, P])
        go = sb("go", [P, 2, EB, UT])
        y = sb("y", [P, 2, T, D])
        yn = sb("yn", [P, 2, T, D])
        hx = sb("hx", [P, NT, ROW])
        h2T = sb("h2T", [P, UT])
        top = sb("top", [P, 2, T, 8])
        top_i = sb("top_i", [P, 2, T, 8], U32)
        first_e = sb("first_e", [P, 2, T, K])
        oh = sb("oh", [P, 2, T, K, E], BF16)
        before = sb("before", [P, U + 1, K, E], BF16)
        in_unit = sb("in_unit", [P, K, E], BF16)
        gap = sb("gap", [P, 2, T])
        lean = sb("lean", [P, 2, T])
        picked = sb("picked", [P, T, K, E])
        place = sb("place", [P, T, K])
        far = sb("far", [P, T, K])
        side = sb("side", [P, T, K])
        base = sb("base", [P, T, K])
        target = sb("target", [P, U, T, K], U32)
        cnt = sb("cnt", [P, K, E])
        cnt_all = sb("cnt_all", [P, E])
        cnt_i = sb("cnt_i", [P, E], I32)
        ends = sb("ends", [P, E])
        one_e = sb("one_e", [P, E])
        start_row = sb("start_row", [P, E])
        pad_row = sb("pad_row", [P, E], I32)
        blk_e = sb("blk_e", [P, NB])
        blk_ei = sb("blk_ei", [P, NB], I32)
        blk_r = sb("blk_r", [P, NB])
        blk_ri = sb("blk_ri", [P, NB], I32)
        is_first = sb("is_first", [P, SLOTS])
        weight = sb("weight", [P, SLOTS])
        dest = sb("dest", [P, SLOTS], U32)
        w1_b = qa
        mtmp = go[:].rearrange("p a e t -> p (a e t)")[:, 0:B * 4 * D].rearrange("p (b g k d) -> p b g k d", b=B, g=2, k=2)
        hid = qb
        xb = go[:].rearrange("p a e t -> p (a e t)")[:, 0:SLOTS * ROW].rearrange("p (s r) -> p s r", s=SLOTS)
        xT = zT[:, 0, 0:2 * P].rearrange("p (s t) -> p s t", s=2)
        yb = y[:].rearrange("p a t d -> p (a t) d")
        cmp = headsT[:].rearrange("p a t -> p (a t)")[:, 0:NB * E].rearrange("p (b e) -> p b e", e=E)
        sel = qk0T[:].rearrange("p a t -> p (a t)")[:, 0:NB * E].rearrange("p (b e) -> p b e", e=E)
        ys_lo = v[:].rearrange("p g t v -> p (g t v)")[:, 0:U // 2 * T * K * D].rearrange(
            "p (u t k d) -> p u t k d", u=U // 2, t=T, k=K)
        ys_hi = gate[:].rearrange("p g e t -> p (g e t)").rearrange("p (u t k d) -> p u t k d", u=U // 2, t=T, k=K)
        ys = [ys_lo[:, u] if u < U // 2 else ys_hi[:, u - U // 2] for u in range(U)]

        bank = [ctx.enter_context(nc.psum_tensor(f"bank{i}", [P, 512], F32)) for i in range(8)]
        p_turn, p_v, p_gate, p_h, p_lkv, p_route = bank[0], bank[1:3], bank[3], bank[4:6], bank[6], bank[7]
        p_po, p_wo, p_sc, p_lk = p_h, p_gate, p_lkv, p_lkv
        p_logit = p_route[:, 0:T * E].rearrange("p (t e) -> p t e", t=T)
        p_count = p_route[:, P:P + T * K * E].rearrange("p (t k e) -> p t k e", t=T, k=K)
        p_total = p_route[:, 2 * P:2 * P + K * E].rearrange("p (k e) -> p k e", k=K)
        p_x, p_hid, p_y = bank[0:2], bank[2:4], bank[4:6]

        const_in = sem("const_in"); mod_in = sem("mod_in"); proj_in = sem("proj_in"); late_in = sem("late_in"); row_in = sem("row_in")
        x_in = [sem(f"x_in{u}") for u in range(U)]
        w1_in = sem("w1_in"); w2_in = sem("w2_in")
        zeroed = sem("zeroed"); halved = sem("halved"); padded = sem("padded"); cleared = sem("cleared")
        tri_ready = sem("tri_ready")
        c_silu = sem("c_silu"); c_spread = sem("c_spread"); mod_copied = sem("mod_copied"); gates_known = sem("gates_known"); mod_done = sem("mod_done"); mod_step = sem("mod_step"); gate_step = sem("gate_step")
        stat_step = sem("stat_step")
        var_ready = [sem(f"var_ready{i}") for i in range(4)]
        rstd_ready = [sem(f"rstd_ready{i}") for i in range(4)]
        nmr_ready = [sem(f"nmr_ready{i}") for i in range(4)]
        xn_ready = sem("xn_ready"); u_half = sem("u_half"); u_ready = sem("u_ready"); z_ready = sem("z_ready")
        z_turned = sem("z_turned"); zt_ready = sem("zt_ready")
        v_done = sem("v_done"); v_biased = sem("v_biased"); v_ready = sem("v_ready")
        gate_done = sem("gate_done"); gate_ready = sem("gate_ready")
        qk_done = sem("qk_done"); qk_silu = sem("qk_silu"); qk_ready = sem("qk_ready"); head_step = sem("head_step")
        heads_ready = sem("heads_ready"); lin_turned = sem("lin_turned"); lin_ready = sem("lin_ready"); turn_in = sem("turn_in")
        t_ready = sem("t_ready")
        lkv_done = sem("lkv_done"); lkv_ready = sem("lkv_ready")
        scores_done = sem("scores_done"); scores_biased = sem("scores_biased"); att_ready = sem("att_ready")
        po_done = sem("po_done"); go_ready = sem("go_ready"); wo_done = sem("wo_done"); y_ready = sem("y_ready")
        yn_ready = sem("yn_ready"); yw_ready = sem("yw_ready"); x_shifted = sem("x_shifted"); x2_ready = sem("x2_ready")
        h2n_ready = sem("h2n_ready"); h2_scaled = sem("h2_scaled"); h2_ready = sem("h2_ready")
        h2_turned = sem("h2_turned"); h2t_ready = sem("h2t_ready")
        logits_done = sem("logits_done"); route_step = sem("route_step"); gap_ready = sem("gap_ready")
        lean_ready = sem("lean_ready"); oh_ready = sem("oh_ready"); before_ready = sem("before_ready"); counted = sem("counted")
        rows_ready = sem("rows_ready"); scattered = sem("scattered")
        totalled = sem("totalled"); pads_known = sem("pads_known"); pads_out = sem("pads_out")
        blocks_ready = sem("blocks_ready")
        block_in = [sem(f"block_in{k}") for k in range(SLOTS)]
        x_turned = sem("x_turned"); xT_ready = sem("xT_ready"); w1_ready = sem("w1_ready")
        hid_done = sem("hid_done"); hid_ready = sem("hid_ready"); y_done = sem("y_done")
        meta_step = sem("meta_step"); meta_ready = sem("meta_ready"); y_scaled = sem("y_scaled")
        y_out = [sem(f"y_out{k}") for k in range(SLOTS)]
        y_in = [sem(f"y_in{u}") for u in range(U)]
        taken = sem("taken"); fin_step = sem("fin_step"); ffn_ready = sem("ffn_ready"); fin_ready = sem("fin_ready"); stored = sem("stored")

        block = ctx.enter_context(nc.Block())

        def after(eng, s, value):
            if value > 0:
                eng.wait_ge(s, value)

        def tiles(u):
            return X[:, T * u:T * u + T, :]

        def features(u):
            return hx[:, T * u:T * u + T, 0:D]

        def blocks(eng, step):
            with eng.Fori(0, GROUPS) as i:
                for k in range(SLOTS):
                    step(i * SLOTS + k, k, i)
            for k in range(NB % SLOTS):
                step(GROUPS * SLOTS + k, k, GROUPS)

        @block.sync
        def _(sp):
            sp.dma_start(X[:, 0:T, :], x[0]).then_inc(x_in[0], 16)
            sp.dma_start(cT[:], c_t).then_inc(mod_in, 16)
            sp.dma_start(wmod_s[:], w_mod).then_inc(mod_in, 16)
            sp.dma_start(X[:, T:2 * T, :], x[1]).then_inc(x_in[1], 16)
            sp.dma_start(row[:], rows.partition_broadcast(P)).then_inc(row_in, 16)
            sp.dma_start(con[:], consts).then_inc(const_in, 16)
            sp.dma_start(col[:], cols).then_inc(proj_in, 16)
            sp.dma_start(wv_s[:], w_v).then_inc(proj_in, 16)
            sp.dma_start(wqk_s[:], w_qk).then_inc(proj_in, 16)
            sp.dma_start(wg_s[:], w_g).then_inc(proj_in, 16)
            for u in range(2, U):
                sp.dma_start(tiles(u), x[u]).then_inc(x_in[u], 16)
                if u == 2:
                    sp.dma_start(turn[:], turns).then_inc(turn_in, 16)
                    sp.dma_start(wo_s[:], w_o).then_inc(late_in, 16)
                    sp.dma_start(wr_s[:], w_r).then_inc(late_in, 16)
                    sp.dma_start(bias_s[:], bias).then_inc(late_in, 16)
            sp.dma_start(w1_s[:], w_1).then_inc(w1_in, 16)
            sp.dma_start(w2_s[:], w_2).then_inc(w2_in, 16)
            sp.wait_ge(padded, 2)
            sp.dma_start(from_experts.rearrange("(p n) d -> p n d", p=P),
                         pad[:, 0:D].unsqueeze(1).to_broadcast([P, K * B * N // P, D])).then_inc(cleared, 16)
            sp.dma_start(to_experts[SPARE:SPARE + P, :], pad[:]).then_inc(pads_out, 16)
            sp.wait_ge(pads_known, 1)
            for e in range(E):
                at = sp.value_load(pad_row[0:1, e:e + 1], min_val=0, max_val=SPARE - P)
                sp.dma_start(to_experts[bass.ds(at, P), :], pad[:]).then_inc(pads_out, 16)
            sp.wait_ge(pads_out, 16 * (E + 1))
            sp.wait_ge(scattered, 16 * K * NT)
            sp.wait_ge(blocks_ready, 1)

            def load(j, k, i):
                sp.wait_ge(meta_ready, j + 1)
                sp.wait_ge(x_turned, j + 1)
                at = sp.value_load(blk_ri[0:1, bass.ds(j, 1)], min_val=0, max_val=SPARE)
                sp.dma_start(xb[:, k, :], to_experts[bass.ds(at, P), :]).then_inc(block_in[k], 16)

            blocks(sp, load)
            for k in range(SLOTS):
                sp.wait_ge(y_out[k], 16 * len(range(k, NB, SLOTS)))
            for u in range(U):
                src = from_experts[K * UT * u:K * UT * (u + 1), :].rearrange("(p r) d -> p (r d)", p=P)
                sp.dma_start(ys[u].rearrange("p t k d -> p (t k d)"), src).then_inc(y_in[u], 16)
            for u in range(U):
                sp.wait_ge(fin_ready, u + 1)
                sp.dma_start(out[u], tiles(u)).then_inc(stored, 16)
            sp.wait_ge(stored, 16 * U)

        @block.gpsimd
        def _(pool):
            for s, n in ((meta_ready, SLOTS), (x_turned, SLOTS), (xT_ready, 2), (hid_ready, 2), (hid_done, 2),
                         (y_scaled, 2), (y_done, 2)):
                pool.sem_inc(s, n)
            pool.memset(half[:], -0.5).then_inc(halved, 1)
            pool.memset(pad[:], 0.0).then_inc(padded, 1)
            pool.memset(qk0T[:], 0.0).then_inc(zeroed, 1)
            pool.memset(lkv[:], 0.0).then_inc(zeroed, 1)
            pool.memset(att[:], 0.0).then_inc(zeroed, 1)
            pool.memset(ones16[:], 1.0).then_inc(zeroed, 1)
            pool.memset(before[:, 0], 0.0).then_inc(zeroed, 1)
            pool.wait_ge(halved, 1)
            pool.wait_ge(padded, 1)
            pool.memset(pad[:, D:D + 1], float(NOWHERE)).then_inc(padded, 1)

            def inverse_root(i, u):
                pool.wait_ge(var_ready[i], u + 1)
                pool.tensor_tensor(rstd[:, i, u % 2, :], var[:, i, u % 2, :], half[:], ALU.pow)\
                    .then_inc(rstd_ready[i], 1)
                pool.wait_ge(rstd_ready[i], u + 1)
                pool.tensor_tensor(nmr[:, i, u % 2, :], minus[:, i, u % 2, :], rstd[:, i, u % 2, :], ALU.mult)\
                    .then_inc(nmr_ready[i], 1)

            def scatter(u, tiles_of_half):
                pool.wait_ge(rows_ready, u + 1)
                for t in tiles_of_half:
                    for k in range(K):
                        pool.indirect_dma_start(
                            out=to_experts, out_offset=bass.IndirectOffsetOnAxis(ap=target[:, u, t, k:k + 1], axis=0),
                            in_=hx[:, T * u + t, :], in_offset=None, bounds_check=SPARE - 1, oob_is_err=False)\
                            .then_inc(scattered, 16)

            for step, u in order():
                b = u // UB
                if step == "root_x":
                    inverse_root(0, u)
                elif step == "modulate_x":
                    pool.wait_ge(xn_ready, u + 1)
                    pool.wait_ge(mod_done, 1)
                    pool.tensor_tensor(xn[:, u % 2], xn[:, u % 2], mod[:, b, 1:2, :].to_broadcast([P, T, D]), ALU.mult)\
                        .then_inc(u_half, 1)
                    pool.wait_ge(u_half, u + 1)
                    pool.tensor_tensor(xn[:, u % 2], xn[:, u % 2], mod[:, b, 0:1, :].to_broadcast([P, T, D]), ALU.add)\
                        .then_inc(u_ready, 1)
                elif step == "root_u":
                    inverse_root(1, u)
                elif step == "shift_x":
                    pool.wait_ge(xn_ready, u + 1)
                    pool.wait_ge(gates_known, 1)
                    pool.tensor_tensor(tiles(u), tiles(u), ln2b[:, b:b + 1, :].to_broadcast([P, T, D]), ALU.add)\
                        .then_inc(x_shifted, 1)
                elif step == "root_y":
                    inverse_root(2, u)
                elif step == "root_x2":
                    inverse_root(3, u)
                elif step == "scatter_a":
                    scatter(u, range(T // 2))
                elif step == "scatter_b":
                    scatter(u, range(T // 2, T))

            def scatter_block(j, k, i):
                pool.wait_ge(y_scaled, j + 1 + 2)
                pool.sem_inc(taken, 1)
                pool.indirect_dma_start(
                    out=from_experts, out_offset=bass.IndirectOffsetOnAxis(ap=dest[:, k:k + 1], axis=0),
                    in_=yb[:, k, :], in_offset=None, bounds_check=K * B * N - 1, oob_is_err=False)\
                    .then_inc(y_out[k], 16)

            pool.wait_ge(cleared, 16)
            blocks(pool, scatter_block)
            for u in range(U):
                pool.wait_ge(ffn_ready, u + 1)
                pool.tensor_tensor(tiles(u), tiles(u), ys[u][:, :, 0, :], ALU.add).then_inc(fin_ready, 1)

        @block.scalar
        def _(act):
            act.wait_ge(mod_in, 32)
            act.activation(sc[:], cT[:], ACT.Silu).then_inc(c_silu, 1)

            def normalise(i, dst, src, u, done):
                act.wait_ge(nmr_ready[i], u + 1)
                for t in range(T):
                    last = act.activation(dst[:, t, :], src[:, t, :], ACT.Identity, bias=nmr[:, i, u % 2, t:t + 1],
                                          scale=rstd[:, i, u % 2, t:t + 1])
                last.then_inc(done, 1)

            def copy_mod(j):
                for b in range(B):
                    act.wait_ge(mod_step, 2 * j + b + 1)
                    act.activation(mod[:, b, 3 * j:3 * j + 3, :],
                                   bank[1 + 3 * b + j][:, 0:3 * D].rearrange("p (k d) -> p k d", k=3), ACT.Copy)\
                        .then_inc(mod_copied, 1)

            copy_mod(0)
            for step, u in order():
                if step == "norm_x":
                    after(act, z_ready, u - 1)
                    normalise(0, xn[:, u % 2], tiles(u), u, xn_ready)
                    if u == 0:
                        copy_mod(1)
                        act.wait_ge(proj_in, 64)
                elif step == "norm_u":
                    after(act, z_turned, u - 1)
                    normalise(1, z[:, u % 2], xn[:, u % 2], u, z_ready)
                elif step == "z_columns":
                    act.wait_ge(z_turned, u + 1)
                    after(act, v_done, T * (u - 1))
                    after(act, qk_done, 2 * (u - 1))
                    act.activation(zT[:, u % 2, :], p_turn[:, :], ACT.Identity, bias=col[:, L_B:L_B + 1], scale=col[:, L_W:L_W + 1])\
                        .then_inc(zt_ready, 1)
                elif step in ("gate_a", "gate_b"):
                    e = int(step == "gate_b")
                    act.wait_ge(gate_done, EB * u + e + 1)
                    after(act, go_ready, u - UB + 1)
                    act.activation(gate[:, u % UB, e, :], p_gate[:, :], ACT.Silu, bias=col[:, L_BG + e:L_BG + e + 1])\
                        .then_inc(gate_ready, 1)
                elif step == "silu_v":
                    act.wait_ge(v_biased, 2 * (u + 1))
                    act.activation(v[:, u % UB], v[:, u % UB], ACT.Silu).then_inc(v_ready, 1)
                elif step == "silu_qk":
                    act.wait_ge(qk_done, 2 * u + 2)
                    after(act, heads_ready, u - 1)
                    for i, dst in ((0, qa), (1, qb)):
                        act.activation(dst[:, u % 2, :], p_h[i][:, :], ACT.Silu, bias=col[:, L_BQ + i:L_BQ + i + 1])\
                            .then_inc(qk_silu, 1)
                    for i, dst in ((0, qa), (1, qb)):
                        act.wait_ge(qk_silu, 2 * u + i + 1)
                        act.activation(dst[:, u % 2, :], dst[:, u % 2, :], ACT.Identity,
                                       bias=col[:, L_BET + i:L_BET + i + 1],
                                       scale=col[:, L_GAM + i:L_GAM + i + 1]).then_inc(qk_ready, 1)
                elif step == "quad_k":
                    act.wait_ge(heads_ready, u + 1)
                    after(act, scores_done, u - UB + 1)
                    act.activation(qk0T[0:QK, u % UB, :], headsT[2 * QK:3 * QK, u % UB, :], ACT.Copy)\
                        .then_inc(t_ready, 1)
                elif step == "lin_k":
                    act.wait_ge(lin_turned, u + 1)
                    after(act, lkv_done, u - 1)
                    act.activation(lin_k[:, u % 2], p_lk[:, :].rearrange("p (t d) -> p t d", t=T)[:, :, 3 * QK:4 * QK],
                                   ACT.Copy).then_inc(lin_ready, 1)
                elif step == "norm_y":
                    after(act, x2_ready, u - 1)
                    normalise(2, yn[:, u % 2], y[:, u % 2], u, yn_ready)
                elif step == "norm_x2":
                    normalise(3, features(u), tiles(u), u, h2n_ready)
                elif step == "h_columns":
                    act.wait_ge(h2_turned, u + 1)
                    after(act, logits_done, u)
                    act.activation(h2T[:, :], p_turn[:, :], ACT.Copy).then_inc(h2t_ready, 1)
                elif step == "lean":
                    act.wait_ge(gap_ready, u + 1)
                    act.activation(lean[:, u % 2, :], gap[:, u % 2, :], ACT.Tanh, scale=0.5).then_inc(lean_ready, 1)

            def gelu(j, k, i):
                act.wait_ge(hid_done, j + 1 + 2)
                act.wait_ge(y_done, j + 1)
                act.activation(hid[:, k % 2, :], p_hid[k % 2][:, :], ACT.Gelu).then_inc(hid_ready, 1)

            blocks(act, gelu)

        @block.vector
        def _(dve):
            dve.wait_ge(c_silu, 1)
            dve.tensor_copy(c_rep[:], sc[:, :].unsqueeze(2).to_broadcast([P, B, P])).then_inc(c_spread, 1)

            def mod_scale(j):
                dve.wait_ge(mod_copied, 2 * j + 2)
                dve.tensor_scalar(mod[:, :, 3 * j + 1, :], mod[:, :, 3 * j + 1, :], 1.0, None, ALU.add)\
                    .then_inc(mod_done, 1)

            def mod_gates():
                mod_scale(1)
                dve.wait_ge(row_in, 16)
                dve.tensor_scalar(mtmp[:, :, :, 0, :], mod[:, :, 2::3, :], 0.0, 2.0, ALU.is_ge, ALU.mult)
                for b in range(B):
                    last = dve.scalar_tensor_tensor(out=mtmp[:, b, :, 1, :], in0=mod[:, b, 2::3, :], scalar=-1.0,
                                                    in1=mod[:, b, 2::3, :], op0=ALU.mult, op1=ALU.max)
                last.then_inc(gate_step, 1)
                dve.wait_ge(gate_step, 1)
                dve.tensor_scalar(mtmp[:, :, :, 1, :], mtmp[:, :, :, 1, :], 0.25, None, ALU.max).then_inc(gate_step, 1)
                dve.wait_ge(gate_step, 2)
                for b in range(B):
                    last = dve.scalar_tensor_tensor(out=mod[:, b, 2::3, :], in0=mtmp[:, b, :, 0, :], scalar=-1.0,
                                                    in1=mtmp[:, b, :, 1, :], op0=ALU.add, op1=ALU.mult)
                last.then_inc(gate_step, 1)
                dve.wait_ge(gate_step, 3)
                for vector, at in ((ln2w, R_W2), (ln2b, R_B2)):
                    last = dve.tensor_tensor(vector[:], mod[:, :, 2, :],
                                             row[:, at:at + D].unsqueeze(1).to_broadcast([P, B, D]), ALU.mult)
                last.then_inc(gates_known, 1)

            count = {"stat": 0, "route": 0}

            def then_stat(ins):
                count["stat"] += 1
                ins.then_inc(stat_step, 1)
                dve.wait_ge(stat_step, count["stat"])

            def then_route(ins):
                count["route"] += 1
                ins.then_inc(route_step, 1)
                dve.wait_ge(route_step, count["route"])

            def variance(i, src, u):
                after(dve, (xn_ready, z_ready, yn_ready, h2n_ready)[i], u - 1)
                for t in range(T):
                    last = dve.bn_stats(stats[:, i, u % 2, t, :], src[:, t, :])
                then_stat(last)
                for t in range(T):
                    last = dve.bn_aggr(mv[:, i, u % 2, t, :], stats[:, i, u % 2, t, :])
                then_stat(last)
                dve.tensor_scalar(minus[:, i, u % 2, :], mv[:, i, u % 2, :, 0], -1.0, None, ALU.mult)
                dve.tensor_scalar(var[:, i, u % 2, :], mv[:, i, u % 2, :, 1], EPS, None, ALU.add)\
                    .then_inc(var_ready[i], 1)

            def bias_v(u, e):
                after(dve, po_done, u - UB + 1)
                dve.wait_ge(v_done, T * u + 2 * e + 2)
                dve.tensor_tensor(v[:, u % UB, 2 * e:2 * e + 2, :], p_v[e][:, :].rearrange("p (t h) -> p t h", t=2),
                                  row[:, R_BV:R_BV + H].unsqueeze(1).to_broadcast([P, 2, H]), ALU.add)\
                    .then_inc(v_biased, 1)

            def rotate(u):
                at = slice(UT * (u % UB), UT * (u % UB) + UT)
                if u == 0:
                    dve.wait_ge(turn_in, 16)
                after(dve, po_done, u - UB + 1)
                for i, term in ((0, qa), (1, qb)):
                    dve.wait_ge(qk_ready, 2 * u + i + 1)
                    dve.tensor_tensor(term[:, u % 2, :], term[:, u % 2, :], turn[:, i, at], ALU.mult)\
                        .then_inc(head_step, 1)
                dve.wait_ge(head_step, 2 * u + 2)
                dve.tensor_tensor(headsT[:, u % UB, :], qa[:, u % 2, :], qb[:, u % 2, :], ALU.add)\
                    .then_inc(heads_ready, 1)

            def square_relu(u):
                dve.wait_ge(scores_done, u + 1)
                after(dve, att_ready, u)
                after(dve, po_done, u - 1)
                for a in range(2):
                    last = dve.scalar_tensor_tensor(
                        out=att1[G * a:G * a + G], scalar=1.0 / G,
                        in0=p_sc[G * a:G * a + G, :].rearrange("p (t i) -> p t i", t=T)[:, :, G * a:G * a + G],
                        in1=bias_s[G * a:G * a + G, :].unsqueeze(1).to_broadcast([G, T, G]),
                        op0=ALU.mult, op1=ALU.add)
                last.then_inc(scores_biased, 1)
                dve.wait_ge(scores_biased, u + 1)
                for a in range(2):
                    last = dve.scalar_tensor_tensor(
                        out=att[G * a:G * a + G, u % 2, :, G * a:G * a + G], in0=att1[G * a:G * a + G], scalar=0.0,
                        in1=att1[G * a:G * a + G], op0=ALU.max, op1=ALU.mult)
                last.then_inc(att_ready, 1)

            def gated(u):
                dve.wait_ge(po_done, u + 1)
                dve.wait_ge(gate_ready, EB * (u + 1))
                after(dve, wo_done, u - 1)
                for e in range(EB):
                    last = dve.tensor_tensor(go[:, u % 2, e, :], p_po[e][:, :], gate[:, u % UB, e, :], ALU.mult)
                last.then_inc(go_ready, 1)

            def bias_out(u):
                dve.wait_ge(wo_done, u + 1)
                after(dve, yn_ready, u - 1)
                dve.tensor_tensor(y[:, u % 2], p_wo[:, :].rearrange("p (t d) -> p t d", t=T),
                                  row[:, R_BO:R_BO + D].unsqueeze(1).to_broadcast([P, T, D]), ALU.add)\
                    .then_inc(y_ready, 1)
                dve.wait_ge(y_ready, u + 1)
                variance(2, y[:, u % 2], u)

            def choose(u):
                s = u % 2
                dve.wait_ge(logits_done, u + 1)
                after(dve, rows_ready, u - 1)
                for t in range(T):
                    last = dve.max(top[:, s, t, :], p_logit[:, t, :])
                then_route(last)
                for t in range(T):
                    last = dve.max_index(top_i[:, s, t, :], top[:, s, t, :], p_logit[:, t, :])
                dve.tensor_tensor(gap[:, s, :], top[:, s, :, 1], top[:, s, :, 0], ALU.subtract).then_inc(gap_ready, 1)
                dve.wait_ge(gap_ready, u + 1)
                then_route(dve.tensor_copy(first_e[:, s], top_i[:, s, :, 0:K]))
                dve.tensor_tensor(oh[:, s], expert_no.unsqueeze(1).unsqueeze(1).to_broadcast([P, T, K, E]),
                                  first_e[:, s].unsqueeze(3).to_broadcast([P, T, K, E]), ALU.is_equal)\
                    .then_inc(oh_ready, 1)
                dve.wait_ge(oh_ready, u + 1)
                with nc.allow_low_precision("counts of up to T are exact"):
                    then_route(dve.tensor_reduce(in_unit[:], oh[:, s].rearrange("p t k e -> p k e t"), AX.X, ALU.add))
                dve.tensor_tensor(before[:, u + 1], before[:, u], in_unit[:], ALU.add).then_inc(before_ready, 1)
                dve.wait_ge(before_ready, u + 1)

            def rows_of(u):
                s = u % 2
                dve.wait_ge(counted, u + 1)
                then_route(dve.tensor_tensor(picked[:], p_count, oh[:, s], ALU.mult))
                then_route(dve.tensor_reduce(place[:], picked[:], AX.X, ALU.add))
                dve.tensor_scalar(far[:], place[:], float(CAP), float(NOWHERE), ALU.is_gt, ALU.mult)
                dve.tensor_scalar(side[:, :, 0], place[:, :, 0], -1.0, None, ALU.add)
                dve.tensor_scalar(side[:, :, 1], place[:, :, 1], -1.0, None, ALU.mult)
                then_route(dve.tensor_scalar(base[:], first_e[:, s], float(PITCH), float(CAP), ALU.mult, ALU.add))
                then_route(dve.tensor_tensor(base[:], base[:], side[:], ALU.add))
                dve.tensor_tensor(target[:, u], base[:], far[:], ALU.add)
                mark = hx[:, T * u:T * u + T, D:ROW]
                dve.wait_ge(lean_ready, u + 1)
                dve.tensor_copy(mark[:, :, 0], token_mark[:, T * u:T * u + T])
                dve.tensor_scalar(mark[:, :, 1], lean[:, s, :], 0.5, 0.5, ALU.mult, ALU.add)
                dve.tensor_scalar(mark[:, :, 2], lean[:, s, :], -1.0, None, ALU.mult)
                dve.tensor_copy(mark[:, :, 3], first_e[:, s, :, 0]).then_inc(rows_ready, 1)

            dve.wait_ge(x_in[0], 16)

            for step, u in order():
                if step == "stats_x":
                    dve.wait_ge(x_in[u], 16)
                    variance(0, tiles(u), u)
                    if u == 0:
                        mod_scale(0)
                        dve.wait_ge(const_in, 16)
                        dve.tensor_copy(tri16[:], con[:, C_TRI:C_TRI + P]).then_inc(tri_ready, 1)
                        dve.wait_ge(zeroed, 5)
                elif step == "stats_u":
                    dve.wait_ge(u_ready, u + 1)
                    variance(1, xn[:, u % 2], u)
                elif step == "bias_a":
                    bias_v(u, 0)
                elif step == "bias_b":
                    bias_v(u, 1)
                elif step == "mod_gates":
                    mod_gates()
                elif step == "rotate":
                    rotate(u)
                elif step == "sum_lkv":
                    dve.wait_ge(lkv_done, u + 1)
                    total = lkv[QK:2 * QK, u // UB, :]
                    if u % UB == 0:
                        dve.tensor_scalar(total, p_lkv[QK:2 * QK, 0:H], 1.0 / N, None, ALU.mult).then_inc(lkv_ready, 1)
                    else:
                        dve.wait_ge(lkv_ready, u)
                        dve.scalar_tensor_tensor(out=total, in0=p_lkv[QK:2 * QK, 0:H], scalar=1.0 / N, in1=total,
                                                 op0=ALU.mult, op1=ALU.add).then_inc(lkv_ready, 1)
                elif step == "square":
                    square_relu(u)
                elif step == "gated":
                    gated(u)
                elif step == "bias_y":
                    bias_out(u)
                elif step == "weigh_y":
                    dve.wait_ge(yn_ready, u + 1)
                    dve.wait_ge(gates_known, 1)
                    dve.tensor_tensor(yn[:, u % 2], yn[:, u % 2], ln2w[:, u // UB:u // UB + 1, :].to_broadcast([P, T, D]),
                                      ALU.mult).then_inc(yw_ready, 1)
                elif step == "add_y":
                    dve.wait_ge(yw_ready, u + 1)
                    dve.wait_ge(x_shifted, u + 1)
                    dve.tensor_tensor(tiles(u), tiles(u), yn[:, u % 2], ALU.add).then_inc(x2_ready, 1)
                elif step == "stats_x2":
                    dve.wait_ge(x2_ready, u + 1)
                    variance(3, tiles(u), u)
                elif step == "scale_h":
                    dve.wait_ge(h2n_ready, u + 1)
                    dve.tensor_tensor(features(u), features(u),
                                      mod[:, u // UB, 4:5, :].to_broadcast([P, T, D]), ALU.mult)\
                        .then_inc(h2_scaled, 1)
                elif step == "shift_h":
                    dve.wait_ge(h2_scaled, u + 1)
                    dve.tensor_tensor(features(u), features(u), mod[:, u // UB, 3:4, :].to_broadcast([P, T, D]),
                                      ALU.add).then_inc(h2_ready, 1)
                elif step == "choose":
                    choose(u)
                elif step == "rows":
                    rows_of(u)

            dve.wait_ge(totalled, 1)
            then_route(dve.tensor_scalar(cnt[:], p_total, float(CAP), None, ALU.min))
            dve.memset(one_e[:], 1.0)
            dve.tensor_tensor(pad_row[:], expert_row, cnt[:, 0], ALU.add).then_inc(pads_known, 1)
            then_route(dve.tensor_tensor(cnt_all[:], cnt[:, 0], cnt[:, 1], ALU.add))
            then_route(dve.tensor_scalar(cnt_i[:], cnt_all[:], float(P - 1), None, ALU.add))
            then_route(dve.tensor_scalar(cnt_i[:], cnt_i[:], P.bit_length() - 1, None, ALU.logical_shift_right))
            then_route(dve.tensor_copy(cnt_all[:], cnt_i[:]))
            then_route(dve.tensor_tensor_scan(ends[:], one_e[:], cnt_all[:], 0.0, ALU.mult, ALU.add))
            then_route(dve.tensor_tensor(start_row[:], cnt_all[:], ends[:], ALU.subtract))
            then_route(dve.scalar_tensor_tensor(out=start_row[:], in0=start_row[:], scalar=float(P),
                                                in1=expert_row, op0=ALU.mult, op1=ALU.add))
            then_route(dve.tensor_tensor(start_row[:], start_row[:], cnt[:, 1], ALU.subtract))
            then_route(dve.tensor_scalar(blk_r[:], block_row, float(SPARE), 1.0 / P, ALU.add, ALU.mult))
            then_route(dve.tensor_tensor(cmp, ends[:].unsqueeze(1).to_broadcast([P, NB, E]),
                                         blk_r[:].unsqueeze(2).to_broadcast([P, NB, E]), ALU.is_le))
            then_route(dve.tensor_reduce(blk_e[:], cmp, AX.X, ALU.add))
            then_route(dve.tensor_tensor(sel, expert_no.unsqueeze(1).to_broadcast([P, NB, E]),
                                         blk_e[:].unsqueeze(2).to_broadcast([P, NB, E]), ALU.is_equal))
            then_route(dve.tensor_tensor(sel, sel, start_row[:].unsqueeze(1).to_broadcast([P, NB, E]), ALU.mult))
            dve.tensor_scalar(blk_ei[:], blk_e[:], float(E - 1), None, ALU.min)
            then_route(dve.tensor_reduce(blk_r[:], sel, AX.X, ALU.add))
            then_route(dve.scalar_tensor_tensor(out=cmp[:, :, 0], in0=blk_e[:], scalar=float(E), in1=block_row,
                                                op0=ALU.is_lt, op1=ALU.mult))
            then_route(dve.tensor_tensor(blk_r[:], blk_r[:], cmp[:, :, 0], ALU.add))
            dve.tensor_scalar(blk_ri[:], blk_r[:], float(SPARE), None, ALU.add).then_inc(blocks_ready, 1)
            dve.wait_ge(blocks_ready, 1)
            dve.wait_ge(w1_in, 16)

            regs = [dve.alloc_register(f"expert_of{k}") for k in range(SLOTS)]

            def expert_front(j, k, reg):
                e = dve.snap(regs[reg], min_val=0, max_val=E - 1)
                dve.wait_ge(hid_done, j + 1)
                dve.tensor_copy(w1_b[:, k % 2, :], w1_s[:, bass.ds(e, 1), :].rearrange("p e f -> p (e f)"))\
                    .then_inc(w1_ready, 1)
                dve.wait_ge(x_turned, j + 1 + SLOTS)
                dve.tensor_copy(xT[:, k % 2, :], p_x[k % 2][:, 0:P]).then_inc(xT_ready, 1)

            def meta(j, k, i, first=False):
                dve.wait_ge(block_in[k], 16 * i + 16)
                if not first:
                    dve.wait_ge(y_out[k], 16 * i)
                dve.tensor_tensor(is_first[:, k:k + 1], xb[:, k, D + 3:D + 4], blk_e[:, bass.ds(j, 1)],
                                  ALU.is_equal).then_inc(meta_step, 1)
                dve.wait_ge(meta_step, j + 1)
                dve.scalar_tensor_tensor(out=weight[:, k:k + 1], in0=is_first[:, k:k + 1],
                                         scalar=xb[:, k, D + 2:D + 3], in1=xb[:, k, D + 1:D + 2],
                                         op0=ALU.mult, op1=ALU.add)
                dve.tensor_tensor(dest[:, k:k + 1], xb[:, k, D:D + 1], is_first[:, k:k + 1], ALU.subtract)\
                    .then_inc(meta_ready, 1)
                dve.wait_ge(meta_ready, j + 1 + SLOTS)

            def scale_out(j, k):
                dve.wait_ge(y_done, j + 1 + 2)
                dve.tensor_scalar(yb[:, k, :], p_y[k % 2][:, 0:D], weight[:, k:k + 1], None, ALU.mult)\
                    .then_inc(y_scaled, 1)

            dve.load(regs, blk_ei[0:1, 0:SLOTS])
            for k in range(2):
                expert_front(k, k, k)
            def group(i, first=False):
                dve.load(regs, blk_ei[0:1, 2:2 + SLOTS] if first else blk_ei[0:1, bass.ds(i * SLOTS + 2, SLOTS)])
                for k in range(SLOTS):
                    j = i * SLOTS + k
                    expert_front(j + 2, (k + 2) % SLOTS, k)
                    meta(j, k, i, first)
                    scale_out(j, k)

            group(0, first=True)
            with dve.Fori(1, GROUPS) as i:
                group(i)
            dve.load(regs, blk_ei[0:1, LAST:NB])
            for j in range(GROUPS * SLOTS, NB):
                if j + 2 < NB:
                    expert_front(j + 2, (j + 2) % SLOTS, j + 2 - LAST)
                meta(j, j % SLOTS, j // SLOTS)
                scale_out(j, j % SLOTS)

            for u in range(U):
                dve.wait_ge(y_in[u], 16)
                dve.tensor_tensor(ys[u][:, :, 0, :], ys[u][:, :, 0, :], ys[u][:, :, 1, :], ALU.add).then_inc(fin_step, 1)
                dve.wait_ge(fin_step, u + 1)
                dve.tensor_tensor(ys[u][:, :, 0, :], ys[u][:, :, 0, :],
                                  mod[:, u // UB, 5:6, :].to_broadcast([P, T, D]), ALU.mult).then_inc(ffn_ready, 1)

        @block.tensor
        def _(pe):
            pe.wait_ge(c_spread, 1)
            pe.wait_ge(mod_in, 32)
            for j in range(2):
                for b in range(B):
                    pe.matmul(bank[1 + 3 * b + j][:, 0:3 * D], c_rep[:, b, :], wmod_s[:, 3 * D * j:3 * D * (j + 1)],
                              start=True, stop=True).then_inc(mod_step, 1)
            pe.wait_ge(const_in, 16)
            pe.wait_ge(proj_in, 64)
            pe.wait_ge(mod_copied, 4)
            n = dict.fromkeys(("turn_z", "project_qk", "turn_lin_k", "lin_kv", "scores", "attend", "project_out", "turn_h", "logits"), 0)
            gates = 0

            def turn_bank_free():
                after(pe, zt_ready, n["turn_z"])
                after(pe, h2t_ready, n["turn_h"])

            def gate_bank_free():
                after(pe, gate_ready, gates)
                after(pe, y_ready, n["project_out"])

            def head_banks_free():
                after(pe, qk_silu, 2 * n["project_qk"])
                after(pe, go_ready, n["attend"])

            def score_bank_free():
                after(pe, lin_ready, n["turn_lin_k"])
                after(pe, lkv_ready, n["lin_kv"])
                after(pe, scores_biased, n["scores"])

            for step, u in order():
                if step == "turn_z":
                    pe.wait_ge(z_ready, u + 1)
                    turn_bank_free()
                    for t in range(T):
                        last = pe.transpose(p_turn[:, P * t:P * t + P], z[:, u % 2, t, :], ident)
                    last.then_inc(z_turned, 1)
                elif step in ("project_a", "project_b"):
                    e = int(step == "project_b")
                    pe.wait_ge(zt_ready, u + 1)
                    gate_bank_free()
                    pe.matmul(p_gate[:, :], wg_s[:, P * e:P * e + P], zT[:, u % 2, :], start=True, stop=True)\
                        .then_inc(gate_done, 1)
                    gates += 1
                    for t in range(2 * e, 2 * e + 2):
                        after(pe, v_biased, 2 * u + e - 1)
                        pe.matmul(p_v[e][:, H * (t % 2):H * (t % 2) + H], zT[:, u % 2, P * t:P * t + P], wv_s[:],
                                  start=True, stop=True).then_inc(v_done, 1)
                elif step == "project_qk":
                    pe.wait_ge(zt_ready, u + 1)
                    head_banks_free()
                    for i in range(2):
                        pe.matmul(p_h[i][:, :], wqk_s[:, i, :], zT[:, u % 2, :], start=True, stop=True)\
                            .then_inc(qk_done, 1)
                elif step == "turn_lin_k":
                    pe.wait_ge(heads_ready, u + 1)
                    score_bank_free()
                    for t in range(T):
                        last = pe.transpose(p_lk[:, P * t:P * t + P], headsT[:, u % UB, P * t:P * t + P], ident)
                    last.then_inc(lin_turned, 1)
                elif step == "lin_kv":
                    pe.wait_ge(v_ready, u + 1)
                    score_bank_free()
                    for t in range(T):
                        last = pe.matmul(p_lkv[QK:2 * QK, 0:H], lin_k[:, u % 2, t, :], v[:, u % UB, t, :],
                                         start=(t == 0), stop=(t == T - 1))
                    last.then_inc(lkv_done, 1)
                elif step == "scores":
                    pe.wait_ge(t_ready, u + 1)
                    pe.wait_ge(late_in, 48)
                    score_bank_free()
                    for t in range(T):
                        last = pe.matmul(p_sc[:, P * t:P * t + P], qk0T[:, u % UB, P * t:P * t + P],
                                         headsT[:, u % UB, P * t:P * t + P], start=True, stop=True)
                    last.then_inc(scores_done, 1)
                elif step == "attend":
                    b = u // UB
                    pe.wait_ge(lkv_ready, UB * (b + 1))
                    head_banks_free()
                    pe.wait_ge(att_ready, u + 1)
                    for e in range(EB):
                        for t in range(T):
                            tile = p_po[e][:, P * t:P * t + P]
                            pe.matmul(tile, lkv[:, b, P * e:P * e + P], headsT[:, u % UB, P * t:P * t + P],
                                      start=True, stop=False)
                            last = pe.matmul(tile, v[:, u % UB, t, P * e:P * e + P], att[:, u % 2, t, :],
                                             start=False, stop=True)
                    last.then_inc(po_done, 1)
                elif step == "project_out":
                    pe.wait_ge(go_ready, u + 1)
                    gate_bank_free()
                    for t in range(T):
                        for e in range(EB):
                            last = pe.matmul(p_wo[:, P * t:P * t + P], go[:, u % 2, e, P * t:P * t + P], wo_s[:, e, :],
                                             start=(e == 0), stop=(e == EB - 1))
                    last.then_inc(wo_done, 1)
                elif step == "turn_h":
                    pe.wait_ge(h2_ready, u + 1)
                    turn_bank_free()
                    for t in range(T):
                        last = pe.transpose(p_turn[:, P * t:P * t + P], hx[:, T * u + t, 0:D], ident)
                    last.then_inc(h2_turned, 1)
                elif step == "logits":
                    pe.wait_ge(h2t_ready, u + 1)
                    after(pe, rows_ready, u)
                    for t in range(T):
                        last = pe.matmul(p_logit[:, t, :], h2T[:, P * t:P * t + P], wr_s[:], start=True, stop=True)
                    last.then_inc(logits_done, 1)
                elif step == "places":
                    pe.wait_ge(oh_ready, u + 1)
                    pe.wait_ge(tri_ready, 1)
                    after(pe, before_ready, u)
                    per_tile = p_route[:, P:P + T * K * E].rearrange("p (t c) -> p t c", t=T)
                    chosen = oh[:, u % 2].rearrange("p t k e -> p t (k e)")
                    earlier = before[:, u:u + 1].rearrange("p t k e -> p t (k e)")
                    pe.matmul(per_tile, ones16[:], earlier.to_broadcast([P, T, K * E]), start=True, stop=False)
                    for t in range(T - 1):
                        pe.matmul(per_tile[:, t + 1:T, :], ones16[:],
                                  chosen[:, t:t + 1, :].to_broadcast([P, T - 1 - t, K * E]), start=False, stop=False)
                    pe.matmul(per_tile, tri16[:], chosen, start=False, stop=True).then_inc(counted, 1)
                if step in n:
                    n[step] += 1
            pe.wait_ge(rows_ready, U)
            pe.matmul(p_route[:, 2 * P:2 * P + K * E], ones16[:], before[:, U].rearrange("p k e -> p (k e)"),
                      start=True, stop=True).then_inc(totalled, 1)

            pe.wait_ge(w2_in, 16)
            pe.wait_ge(blocks_ready, 1)
            regs = [pe.alloc_register(f"expert_of{k}") for k in range(SLOTS)]

            def turn_x(j, k, loads):
                pe.wait_ge(block_in[k], 16 * loads)
                pe.wait_ge(xT_ready, j + 1)
                pe.transpose(p_x[k % 2][:, 0:P], xb[:, k, 0:D], ident).then_inc(x_turned, 1)

            def first_layer(j, k):
                pe.wait_ge(xT_ready, j + 1 + 2)
                pe.wait_ge(w1_ready, j + 1)
                pe.wait_ge(hid_ready, j + 1)
                for f in range(FB):
                    last = pe.matmul(p_hid[k % 2][:, P * f:P * f + P], w1_b[:, k % 2, P * f:P * f + P], xT[:, k % 2, :],
                                     start=True, stop=True)
                last.then_inc(hid_done, 1)

            def second_layer(j, k, e):
                pe.wait_ge(hid_ready, j + 1 + 2)
                pe.wait_ge(y_scaled, j + 1)
                for f in range(FB):
                    last = pe.matmul(p_y[k % 2][:, 0:D], hid[:, k % 2, P * f:P * f + P],
                                     w2_s[:, bass.ds(e, 1), f, :].rearrange("p e d -> p (e d)"),
                                     start=(f == 0), stop=(f == FB - 1))
                last.then_inc(y_done, 1)

            turn_x(0, 0, 1)
            first_layer(0, 0)
            turn_x(1, 1, 1)
            with pe.Fori(0, GROUPS) as i:
                pe.load(regs, blk_ei[0:1, bass.ts(i, SLOTS)])
                for k in range(SLOTS):
                    j = i * SLOTS + k
                    e = pe.snap(regs[k], min_val=0, max_val=E - 1)
                    first_layer(j + 1, (k + 1) % SLOTS)
                    turn_x(j + 2, (k + 2) % SLOTS, i + 1 + (k + 2) // SLOTS)
                    second_layer(j, k, e)
            pe.load(regs, blk_ei[0:1, LAST:NB])
            for j in range(GROUPS * SLOTS, NB):
                e = pe.snap(regs[j - LAST], min_val=0, max_val=E - 1)
                if j + 1 < NB:
                    first_layer(j + 1, (j + 1) % SLOTS)
                if j + 2 < NB:
                    turn_x(j + 2, (j + 2) % SLOTS, (j + 2) // SLOTS + 1)
                second_layer(j, j % SLOTS, e)


def kernel(**inputs):
    import numpy as np
    import concourse.bacc as bacc
    from concourse import mybir as mb
    from concourse.bass_utils import run_bass_kernel_spmd

    a = {k: np.asarray(v) for k, v in inputs.items()}

    def at(name):
        return a["L0_attn_" + name]

    half = QK // 2
    freq = (np.float32(10000.0) ** (-np.arange(half, dtype=np.float32) / np.float32(half))).astype(np.float32)
    ang = np.arange(N, dtype=np.float32)[:, None] * freq[None, :]
    cos = np.tile(np.concatenate([np.cos(ang), np.cos(ang)], 1).T, (NH, 1))
    sin = np.tile(np.concatenate([-np.sin(ang), np.sin(ang)], 1).T, (NH, 1))
    n = np.arange(NT)[None, :]
    token = n // T * UT + np.arange(P)[:, None] * T + n % T
    consts = np.concatenate([np.eye(P), np.triu(np.ones((P, P))), np.tile(np.arange(E), (P, 1)),
                             2 * token + 1, np.tile(np.arange(NB) * P - SPARE, (P, 1)),
                             np.tile(np.arange(E) * PITCH + CAP, (P, 1))], 1).astype(np.float32)
    rows = np.concatenate([at("bv"), at("bo"), at("ln2_w"), at("ln2_b")])
    swapped = np.concatenate([np.arange(half, QK), np.arange(half)])
    cols = np.stack([at("ln1_w"), at("ln1_b"), at("bg")[:P], at("bg")[P:],
                     np.tile(at("bqk"), NH), np.tile(at("bqk")[swapped], NH),
                     at("gamma").ravel(), at("gamma")[:, swapped].ravel(),
                     at("beta").ravel(), at("beta")[:, swapped].ravel()], 1)
    i = np.arange(G)
    bias = at("pos_emb")[np.minimum(np.abs(i[:, None] - i[None, :]), at("pos_emb").shape[0] // 2)]
    arrays = {
        "x": at("x").reshape(U, T, P, D).transpose(0, 2, 1, 3),
        "consts": consts,
        "rows": rows,
        "cols": cols,
        "bias": np.concatenate([bias, bias], 0),
        "c_t": a["L0_c"].T,
        "w_mod": a["L0_wmod"],
        "turns": np.stack([cos, sin], 1).astype(np.float32),
        "w_v": at("Wv").T,
        "w_qk": np.stack([np.tile(at("Wqk").T, (1, NH)), np.tile(at("Wqk")[swapped].T, (1, NH))], 1),
        "w_g": at("Wg").T,
        "w_o": at("Wo").T.reshape(EB, P, D).transpose(1, 0, 2),
        "w_r": a["L0_ffn_router_w"].T,
        "w_1": a["L0_ffn_w1"].transpose(1, 0, 2),
        "w_2": a["L0_ffn_w2"].reshape(E, FB, P, D).transpose(2, 0, 1, 3),
    }
    arrays = {k: np.ascontiguousarray(v) for k, v in arrays.items()}
    nc = bacc.Bacc("TRN2", target_bir_lowering=False, num_devices=1)
    args = [nc.dram_tensor(k, v.shape, mb.dt.from_np(v.dtype), kind="ExternalInput").ap() for k, v in arrays.items()]
    out = nc.dram_tensor("out", (U, P, T, D), mb.dt.float32, kind="ExternalOutput").ap()
    build(nc, *args, out)
    r = run_bass_kernel_spmd(nc, [arrays], core_ids=[0])
    return r.results[0]["out"].reshape(U, P, T, D).transpose(0, 2, 1, 3).reshape(B, N, D)
```
